# Optimizing a Trainium2 kernel written in Bass

```python
import numpy as np
import jax
import jax.numpy as jnp

def _softmax(x, axis=-1):
    return jax.nn.softmax(x, axis=axis)
def _gelu(x):
    return jax.nn.gelu(x, approximate=True)
def _silu(x):
    return jax.nn.silu(x)
def _sigmoid(x):
    return jax.nn.sigmoid(x)
def _layernorm(x, axis=-1, eps=1e-5):
    m = jnp.mean(x, axis=axis, keepdims=True)
    v = jnp.var(x, axis=axis, keepdims=True)
    return (x - m) / jnp.sqrt(v + eps)
def _scatter_add(tgt, idx, src, axis=0):
    return tgt.at[idx].add(src)
def _segment_sum(src, seg, n):
    return jax.ops.segment_sum(src, seg, n)

kernel_name = 'mk_conv_seq_d1_conv_nchw256_6aa2d3'

def setup_inputs(seed: int = 0):
    np.random.seed(seed)
    _w = jnp.asarray
    def _rec_inputs():
        import jax
        import jax.numpy as jnp
        _gk = jax.random.key(seed)
        x = -8.015e-05 + 0.9999 * jax.random.normal(jax.random.fold_in(_gk, 1), (8, 256, 160, 160), jnp.float32)
        return x
    x = _rec_inputs()
    def _L0_conv_setup():
        import jax, jax.numpy as jnp
        import numpy as np
        from jax import lax
        EPS = 1e-05
        IC = 32

        def bn(x, g, b, m, v):
            sh = (1, -1, 1, 1)
            return (x - m.reshape(sh)) * (g.reshape(sh) * lax.rsqrt(v.reshape(sh) + EPS)) + b.reshape(sh)

        def prelu(x, a):
            return jnp.where(x >= 0, x, a * x)

        def conv1x1(x, w):
            return jnp.einsum('bchw,oc->bohw', x, w)

        def dconv(x, w, d):
            return lax.conv_general_dilated(x, w, (1, 1), [(d, d), (d, d)], rhs_dilation=(d, d), dimension_numbers=('NCHW', 'OIHW', 'NCHW'))

        def glca_forward(feature, q_w, q_gamma, q_beta, q_mean, q_var, q_alpha, k_w, k_gamma, k_beta, k_mean, k_var, k_alpha, v_w, v_gamma, v_beta, v_mean, v_var, v_alpha, d1_w, d1_gamma, d1_beta, d1_mean, d1_var, d2_w, d2_gamma, d2_beta, d2_mean, d2_var, d3_w, d3_gamma, d3_beta, d3_mean, d3_var, o_w, o_gamma, o_beta, o_mean, o_var, o_alpha):
            B, C, H, W = feature.shape
            q = prelu(bn(conv1x1(feature, q_w), q_gamma, q_beta, q_mean, q_var), q_alpha)
            k = prelu(bn(conv1x1(feature, k_w), k_gamma, k_beta, k_mean, k_var), k_alpha)
            val = prelu(bn(conv1x1(feature, v_w), v_gamma, v_beta, v_mean, v_var), v_alpha)
            qr = q.transpose(0, 3, 2, 1).reshape(B * W, H, IC)
            kr = k.transpose(0, 3, 1, 2).reshape(B * W, IC, H)
            att = jax.nn.softmax(jnp.matmul(qr, kr), axis=-1)
            branches = []
            for w, g, b, m, var, d in ((d1_w, d1_gamma, d1_beta, d1_mean, d1_var, 1), (d2_w, d2_gamma, d2_beta, d2_mean, d2_var, 3), (d3_w, d3_gamma, d3_beta, d3_mean, d3_var, 5)):
                t = jax.nn.relu(bn(dconv(val, w, d), g, b, m, var))
                t = t.transpose(0, 3, 1, 2).reshape(B * W, H, IC)
                branches.append(jnp.matmul(att, t))
            res = jnp.concatenate(branches, axis=0).reshape(B, W, H, 3 * IC)
            res = res.transpose(0, 3, 2, 1)
            out = prelu(bn(conv1x1(res, o_w), o_gamma, o_beta, o_mean, o_var) + feature, o_alpha)
            return out
        B, C, H, W = (8, 256, 160, 160)
        key = jax.random.key(seed)
        ks = iter(jax.random.split(key, 48))
        d = {}
        d['feature'] = jax.random.normal(next(ks), (B, C, H, W), jnp.float32)
        for p in ('q', 'k', 'v'):
            d[p + '_w'] = jax.random.normal(next(ks), (IC, C), jnp.float32) * 0.05
            d[p + '_gamma'] = jax.random.uniform(next(ks), (IC,), jnp.float32, 0.5, 1.5)
            d[p + '_beta'] = jax.random.normal(next(ks), (IC,), jnp.float32) * 0.1
            d[p + '_mean'] = jax.random.normal(next(ks), (IC,), jnp.float32) * 0.1
            d[p + '_var'] = jax.random.uniform(next(ks), (IC,), jnp.float32, 0.5, 1.5)
            d[p + '_alpha'] = jnp.full((1,), 0.25, jnp.float32)
        for p in ('d1', 'd2', 'd3'):
            d[p + '_w'] = jax.random.normal(next(ks), (IC, IC, 3, 3), jnp.float32) * 0.05
            d[p + '_gamma'] = jax.random.uniform(next(ks), (IC,), jnp.float32, 0.5, 1.5)
            d[p + '_beta'] = jax.random.normal(next(ks), (IC,), jnp.float32) * 0.1
            d[p + '_mean'] = jax.random.normal(next(ks), (IC,), jnp.float32) * 0.1
            d[p + '_var'] = jax.random.uniform(next(ks), (IC,), jnp.float32, 0.5, 1.5)
        d['o_w'] = jax.random.normal(next(ks), (C, 3 * IC), jnp.float32) * 0.05
        d['o_gamma'] = jax.random.uniform(next(ks), (C,), jnp.float32, 0.5, 1.5)
        d['o_beta'] = jax.random.normal(next(ks), (C,), jnp.float32) * 0.1
        d['o_mean'] = jax.random.normal(next(ks), (C,), jnp.float32) * 0.1
        d['o_var'] = jax.random.uniform(next(ks), (C,), jnp.float32, 0.5, 1.5)
        d['o_alpha'] = jnp.full((1,), 0.25, jnp.float32)
        return d
    _L0_conv_all = _L0_conv_setup()
    _L0_conv_in = {k: v for k, v in _L0_conv_all.items() if k in ('q_w', 'q_gamma', 'q_beta', 'q_mean', 'q_var', 'q_alpha', 'k_w', 'k_gamma', 'k_beta', 'k_mean', 'k_var', 'k_alpha', 'v_w', 'v_gamma', 'v_beta', 'v_mean', 'v_var', 'v_alpha', 'd1_w', 'd1_gamma', 'd1_beta', 'd1_mean', 'd1_var', 'd2_w', 'd2_gamma', 'd2_beta', 'd2_mean', 'd2_var', 'd3_w', 'd3_gamma', 'd3_beta', 'd3_mean', 'd3_var', 'o_w', 'o_gamma', 'o_beta', 'o_mean', 'o_var', 'o_alpha', )}
    del _L0_conv_all

    return {
        "x": x,
        "L0_conv_q_w": _L0_conv_in["q_w"],
        "L0_conv_q_gamma": _L0_conv_in["q_gamma"],
        "L0_conv_q_beta": _L0_conv_in["q_beta"],
        "L0_conv_q_mean": _L0_conv_in["q_mean"],
        "L0_conv_q_var": _L0_conv_in["q_var"],
        "L0_conv_q_alpha": _L0_conv_in["q_alpha"],
        "L0_conv_k_w": _L0_conv_in["k_w"],
        "L0_conv_k_gamma": _L0_conv_in["k_gamma"],
        "L0_conv_k_beta": _L0_conv_in["k_beta"],
        "L0_conv_k_mean": _L0_conv_in["k_mean"],
        "L0_conv_k_var": _L0_conv_in["k_var"],
        "L0_conv_k_alpha": _L0_conv_in["k_alpha"],
        "L0_conv_v_w": _L0_conv_in["v_w"],
        "L0_conv_v_gamma": _L0_conv_in["v_gamma"],
        "L0_conv_v_beta": _L0_conv_in["v_beta"],
        "L0_conv_v_mean": _L0_conv_in["v_mean"],
        "L0_conv_v_var": _L0_conv_in["v_var"],
        "L0_conv_v_alpha": _L0_conv_in["v_alpha"],
        "L0_conv_d1_w": _L0_conv_in["d1_w"],
        "L0_conv_d1_gamma": _L0_conv_in["d1_gamma"],
        "L0_conv_d1_beta": _L0_conv_in["d1_beta"],
        "L0_conv_d1_mean": _L0_conv_in["d1_mean"],
        "L0_conv_d1_var": _L0_conv_in["d1_var"],
        "L0_conv_d2_w": _L0_conv_in["d2_w"],
        "L0_conv_d2_gamma": _L0_conv_in["d2_gamma"],
        "L0_conv_d2_beta": _L0_conv_in["d2_beta"],
        "L0_conv_d2_mean": _L0_conv_in["d2_mean"],
        "L0_conv_d2_var": _L0_conv_in["d2_var"],
        "L0_conv_d3_w": _L0_conv_in["d3_w"],
        "L0_conv_d3_gamma": _L0_conv_in["d3_gamma"],
        "L0_conv_d3_beta": _L0_conv_in["d3_beta"],
        "L0_conv_d3_mean": _L0_conv_in["d3_mean"],
        "L0_conv_d3_var": _L0_conv_in["d3_var"],
        "L0_conv_o_w": _L0_conv_in["o_w"],
        "L0_conv_o_gamma": _L0_conv_in["o_gamma"],
        "L0_conv_o_beta": _L0_conv_in["o_beta"],
        "L0_conv_o_mean": _L0_conv_in["o_mean"],
        "L0_conv_o_var": _L0_conv_in["o_var"],
        "L0_conv_o_alpha": _L0_conv_in["o_alpha"],
    }

def reference(x, L0_conv_q_w, L0_conv_q_gamma, L0_conv_q_beta, L0_conv_q_mean, L0_conv_q_var, L0_conv_q_alpha, L0_conv_k_w, L0_conv_k_gamma, L0_conv_k_beta, L0_conv_k_mean, L0_conv_k_var, L0_conv_k_alpha, L0_conv_v_w, L0_conv_v_gamma, L0_conv_v_beta, L0_conv_v_mean, L0_conv_v_var, L0_conv_v_alpha, L0_conv_d1_w, L0_conv_d1_gamma, L0_conv_d1_beta, L0_conv_d1_mean, L0_conv_d1_var, L0_conv_d2_w, L0_conv_d2_gamma, L0_conv_d2_beta, L0_conv_d2_mean, L0_conv_d2_var, L0_conv_d3_w, L0_conv_d3_gamma, L0_conv_d3_beta, L0_conv_d3_mean, L0_conv_d3_var, L0_conv_o_w, L0_conv_o_gamma, L0_conv_o_beta, L0_conv_o_mean, L0_conv_o_var, L0_conv_o_alpha):
    import jax
    import jax.numpy as jnp
    def _L0_conv_ref(feature, q_w, q_gamma, q_beta, q_mean, q_var, q_alpha, k_w, k_gamma, k_beta, k_mean, k_var, k_alpha, v_w, v_gamma, v_beta, v_mean, v_var, v_alpha, d1_w, d1_gamma, d1_beta, d1_mean, d1_var, d2_w, d2_gamma, d2_beta, d2_mean, d2_var, d3_w, d3_gamma, d3_beta, d3_mean, d3_var, o_w, o_gamma, o_beta, o_mean, o_var, o_alpha):
        import jax, jax.numpy as jnp
        import numpy as np
        from jax import lax
        EPS = 1e-05
        IC = 32

        def bn(x, g, b, m, v):
            sh = (1, -1, 1, 1)
            return (x - m.reshape(sh)) * (g.reshape(sh) * lax.rsqrt(v.reshape(sh) + EPS)) + b.reshape(sh)

        def prelu(x, a):
            return jnp.where(x >= 0, x, a * x)

        def conv1x1(x, w):
            return jnp.einsum('bchw,oc->bohw', x, w)

        def dconv(x, w, d):
            return lax.conv_general_dilated(x, w, (1, 1), [(d, d), (d, d)], rhs_dilation=(d, d), dimension_numbers=('NCHW', 'OIHW', 'NCHW'))

        def glca_forward(feature, q_w, q_gamma, q_beta, q_mean, q_var, q_alpha, k_w, k_gamma, k_beta, k_mean, k_var, k_alpha, v_w, v_gamma, v_beta, v_mean, v_var, v_alpha, d1_w, d1_gamma, d1_beta, d1_mean, d1_var, d2_w, d2_gamma, d2_beta, d2_mean, d2_var, d3_w, d3_gamma, d3_beta, d3_mean, d3_var, o_w, o_gamma, o_beta, o_mean, o_var, o_alpha):
            B, C, H, W = feature.shape
            q = prelu(bn(conv1x1(feature, q_w), q_gamma, q_beta, q_mean, q_var), q_alpha)
            k = prelu(bn(conv1x1(feature, k_w), k_gamma, k_beta, k_mean, k_var), k_alpha)
            val = prelu(bn(conv1x1(feature, v_w), v_gamma, v_beta, v_mean, v_var), v_alpha)
            qr = q.transpose(0, 3, 2, 1).reshape(B * W, H, IC)
            kr = k.transpose(0, 3, 1, 2).reshape(B * W, IC, H)
            att = jax.nn.softmax(jnp.matmul(qr, kr), axis=-1)
            branches = []
            for w, g, b, m, var, d in ((d1_w, d1_gamma, d1_beta, d1_mean, d1_var, 1), (d2_w, d2_gamma, d2_beta, d2_mean, d2_var, 3), (d3_w, d3_gamma, d3_beta, d3_mean, d3_var, 5)):
                t = jax.nn.relu(bn(dconv(val, w, d), g, b, m, var))
                t = t.transpose(0, 3, 1, 2).reshape(B * W, H, IC)
                branches.append(jnp.matmul(att, t))
            res = jnp.concatenate(branches, axis=0).reshape(B, W, H, 3 * IC)
            res = res.transpose(0, 3, 2, 1)
            out = prelu(bn(conv1x1(res, o_w), o_gamma, o_beta, o_mean, o_var) + feature, o_alpha)
            return out
        return glca_forward(feature, q_w, q_gamma, q_beta, q_mean, q_var, q_alpha, k_w, k_gamma, k_beta, k_mean, k_var, k_alpha, v_w, v_gamma, v_beta, v_mean, v_var, v_alpha, d1_w, d1_gamma, d1_beta, d1_mean, d1_var, d2_w, d2_gamma, d2_beta, d2_mean, d2_var, d3_w, d3_gamma, d3_beta, d3_mean, d3_var, o_w, o_gamma, o_beta, o_mean, o_var, o_alpha)

    def _gn(v, G=32, eps=1e-5):
        B_, C_, H_, W_ = v.shape
        g = v.reshape(B_, G, C_ // G, H_, W_)
        m = jnp.mean(g, axis=(2, 3, 4), keepdims=True)
        s = jnp.var(g, axis=(2, 3, 4), keepdims=True)
        return ((g - m) / jnp.sqrt(s + eps)).reshape(v.shape)

    def _ln_c(v, eps=1e-6):
        m = jnp.mean(v, axis=1, keepdims=True)
        s = jnp.var(v, axis=1, keepdims=True)
        return (v - m) / jnp.sqrt(s + eps)

    def _ln_t(v, eps=1e-5):
        m = jnp.mean(v, axis=-1, keepdims=True)
        s = jnp.var(v, axis=-1, keepdims=True)
        return (v - m) / jnp.sqrt(s + eps)

    def _to_tokens(v):
        B_, C_, H_, W_ = v.shape
        return v.reshape(B_, C_, H_ * W_).transpose(0, 2, 1)
    def _from_tokens(t, like):
        B_, C_, H_, W_ = like.shape
        return t.transpose(0, 2, 1).reshape(B_, C_, H_, W_)

    x = _L0_conv_ref(x, L0_conv_q_w, L0_conv_q_gamma, L0_conv_q_beta, L0_conv_q_mean, L0_conv_q_var, L0_conv_q_alpha, L0_conv_k_w, L0_conv_k_gamma, L0_conv_k_beta, L0_conv_k_mean, L0_conv_k_var, L0_conv_k_alpha, L0_conv_v_w, L0_conv_v_gamma, L0_conv_v_beta, L0_conv_v_mean, L0_conv_v_var, L0_conv_v_alpha, L0_conv_d1_w, L0_conv_d1_gamma, L0_conv_d1_beta, L0_conv_d1_mean, L0_conv_d1_var, L0_conv_d2_w, L0_conv_d2_gamma, L0_conv_d2_beta, L0_conv_d2_mean, L0_conv_d2_var, L0_conv_d3_w, L0_conv_d3_gamma, L0_conv_d3_beta, L0_conv_d3_mean, L0_conv_d3_var, L0_conv_o_w, L0_conv_o_gamma, L0_conv_o_beta, L0_conv_o_mean, L0_conv_o_var, L0_conv_o_alpha)
    return x


_drawn_inputs = setup_inputs


def setup_inputs(seed=0):
    import zlib

    import numpy as np

    out = dict(_drawn_inputs(seed))
    spreads = {}
    factors = {'L0_conv_q_beta': 3.767,
     'L0_conv_q_mean': 4.006,
     'L0_conv_k_beta': 8.0,
     'L0_conv_k_mean': 8.0,
     'L0_conv_v_beta': 4.802,
     'L0_conv_v_mean': 27.051,
     'L0_conv_v_var': 196.64,
     'L0_conv_d1_gamma': 18.238,
     'L0_conv_d1_beta': 5.542,
     'L0_conv_d1_mean': 5.272,
     'L0_conv_d1_var': 151.348,
     'L0_conv_d2_gamma': 20.509,
     'L0_conv_d2_beta': 7.208,
     'L0_conv_d2_mean': 5.891,
     'L0_conv_d2_var': 200.0,
     'L0_conv_d3_gamma': 21.542,
     'L0_conv_d3_beta': 7.92,
     'L0_conv_d3_mean': 6.047,
     'L0_conv_d3_var': 200.0,
     'L0_conv_v_w': 3.523,
     'L0_conv_v_gamma': 8.0,
     'L0_conv_d3_w': 2.812}
    for name, (base, spread) in spreads.items():
        noise = np.random.default_rng([zlib.crc32(name.encode()), seed]).standard_normal(out[name].shape)
        drawn = base * np.exp(spread * noise) if base else spread * noise
        out[name] = jnp.asarray(drawn.astype(out[name].dtype))
    for name, factor in factors.items():
        out[name] = (out[name] * factor).astype(out[name].dtype)
    return out
```

```python
from contextlib import ExitStack

import numpy as np

import concourse.bass as bass
from concourse import mybir

F32 = mybir.dt.float32
ALU = mybir.AluOpType
ACT = mybir.ActivationFunctionType
AX_X = mybir.AxisListType.X

B, C, H, W = 8, 256, 160, 160
IC = 32
KT = C // 128
G = 4
WG = W // G
ND = 3
DIL = (1, 3, 5)
PAD = max(DIL)
HP, WP = H + 2 * PAD, W + 2 * PAD
R = 4
NCH = H // R
PX = R * WG
NQ = H // IC
NHB = H // IC
LAG = 4
NA = 128 // IC
NB = ND * IC
NV = NB + 1
HALF = W // 2
LEAD = 3
EPS = 1e-5
NPC = 2 * KT + 1
NPR = 3 * IC + NB + C
NH = NCH // 2
assert NCH == WG and NCH % 2 == 0 and NHB == NA + 1 == NQ and R * WG == W


def build(nc, x, wq, wk, wv, wd1, wd2, wd3, wo, bn_row, bn_col, alpha, out):
    vpad = nc.dram_tensor("v_padded", [B, IC, HP, WP], F32, kind="Internal").ap()
    att = nc.dram_tensor("attended", [ND * B * W, H, IC], F32, kind="Internal").ap()

    x_rows = x.rearrange("b (t p) h w -> b p t (h w)", p=128)
    out_rows = out.rearrange("b (t p) h w -> b p t (h w)", p=128)
    v_bands = vpad.rearrange("b c h w -> (b c) (h w)")

    def to_all_partitions(a):
        return bass.AP(tensor=a.tensor, offset=a.offset, ap=[[0, 128]] + list(a.ap))

    with ExitStack() as ctx:
        def sb(name, shape):
            return ctx.enter_context(nc.sbuf_tensor(name, shape, F32))

        def sem(name):
            return ctx.enter_context(nc.semaphore(name))

        q_img = sb("q_img", [128, WG, H])
        k_img = sb("k_img", [128, WG, H])
        t_img = sb("t_img", [128, WG, ND, H])
        xbuf = sb("xbuf", [128, 2, KT, R * W])
        zbuf = sb("zbuf", [128, 2, KT, R * W])
        rbuf = sb("rbuf", [128, KT * R * W])
        win = sb("win", [128, 2, ND * R * WP])
        vbuf = sb("vbuf", [128, 2, WP])
        qdiag = sb("qdiag", [128, 2, NQ, 128])
        kcol = sb("kcol", [128, 2, H])
        tcol = sb("tcol", [128, 2, NHB, NV])
        tfirst = sb("tfirst", [128, 2, G, NV])
        prob = sb("prob", [128, 2, NQ, H])
        probT = sb("probT", [128, 2, 2 * NQ, 128])
        obuf = sb("obuf", [128, 2, ND, NQ, IC])
        wqkv = sb("wqkv", [128, KT, 3, IC])
        wconv = sb("wconv", [128, ND, 3, IC])
        wout = sb("wout", [NB, C])
        ident = sb("ident", [128, 128])
        quarter = sb("quarter", [128, G])
        signed_quarter = sb("signed_quarter", [128, G])
        nmax = sb("nmax", [128, 2, NQ])
        rden = sb("rden", [128, 2, NQ])
        alphas = sb("alphas", [128, 4])
        colbias = sb("colbias", [128, NPC])
        sign = sb("sign", [128, 4])
        leakbias = sb("leakbias", [128, 3])
        unleak = sb("unleak", [128, 4])

        leak = prob[:, :, 0:3].rearrange("p m n j -> p m (n j)")
        window = win[:, :, :].rearrange("p m (d r w) -> p m d r w", d=ND, r=R)
        ZT = 2 * R * NB
        zt = win[0:HALF, :, 0:ZT].rearrange("p m (f r j) -> p m f r j", f=2, r=R)
        zc = win[0:NB, :, ZT:ZT + R * W]
        NP = NPR + NPC
        scratch = t_img[:, :, :, :].rearrange("p w d h -> p (w d h)")
        prm = scratch[:, 0:4 * NP].rearrange("p (k n) -> p k n", k=4)
        gamma, beta, mean, var = (prm[:, n, :] for n in range(4))
        pinv, proot, ptmp, pscale, pbias = (
            scratch[:, (4 + n) * NP:(5 + n) * NP] for n in range(5))
        zeros = k_img[:, :, :].rearrange("p w h -> p (w h)")[:, 0:PAD * WP]

        ps = [ctx.enter_context(nc.psum_tensor(f"ps{n}", [128, 512], F32)) for n in range(8)]
        qkv_ps = [ps[2], ps[3]]
        conv_ps = [ps[4], ps[5]]
        s_ps = [ps[0], ps[1]]
        pt_ps = [ps[2], ps[3]]
        rg_ps = ps[4]
        pv_ps = ps[5]
        pr_ps = [ps[6], ps[7]]
        SQ = 3

        params_in = sem("params_in")
        weights_in = sem("weights_in")
        setup_dve = sem("setup_dve")
        setup_root = sem("setup_root")
        consts = sem("consts")
        zeros_set = sem("zeros_set")
        waited = sem("waited")
        pads_out = sem("pads_out")
        xa_in = [sem(f"xa_in{m}") for m in (0, 1)]
        qkv_done = sem("qkv_done")
        leak_ready = sem("leak_ready")
        qk_kept = sem("qk_kept")
        v_kept = sem("v_kept")
        v_out = [sem(f"v_out{m}") for m in (0, 1)]
        win_in = [sem(f"win_in{m}") for m in (0, 1)]
        conv_done = sem("conv_done")
        conv_kept = sem("conv_kept")
        qk_staged = sem("qk_staged")
        t_staged = sem("t_staged")
        s_done = sem("s_done")
        max_done = sem("max_done")
        exp_done = sem("exp_done")
        rg_done = sem("rg_done")
        tf_kept = sem("tf_kept")
        pt_done = sem("pt_done")
        pa_kept = sem("pa_kept")
        pt_kept = sem("pt_kept")
        pv_done = sem("pv_done")
        den_done = sem("den_done")
        o_kept = sem("o_kept")
        att_out = [sem(f"att_out{m}") for m in (0, 1)]
        xb_in = [sem(f"xb_in{m}") for m in (0, 1)]
        zt_in = [sem(f"zt_in{m}") for m in (0, 1)]
        z_turned = sem("z_turned")
        zt_turned = sem("zt_turned")
        zc_kept = sem("zc_kept")
        pr_done = sem("pr_done")
        z_added = sem("z_added")
        r_ready = sem("r_ready")
        z_done = sem("z_done")
        z_out = [sem(f"z_out{m}") for m in (0, 1)]

        PAD_DMAS = 2 * (B * IC // 128)
        CONSTS = 7 + G + 4
        SETUP_STEPS = 15 + KT + 5 + 4 * ND + 1
        FIRST = NQ - 1
        CREDIT = {qkv_done: 2, conv_done: 2, zt_turned: 2, s_done: 4, pv_done: 2, v_kept: 2, conv_kept: 2,
                  exp_done: NQ, tf_kept: 1, pa_kept: 1, pt_kept: 2, o_kept: 1, z_added: 8, z_done: 1, pr_done: 1,
                  v_out[0]: 16, v_out[1]: 16, att_out[0]: 16, att_out[1]: 16, z_out[0]: 16, z_out[1]: 16}

        block = ctx.enter_context(nc.Block())

        @block.sync
        def _(sp):
            sp.dma_start(prm[:, :, 0:NPR], to_all_partitions(bn_row)).then_inc(params_in, 16)
            sp.dma_start(prm[:, :, NPR:NP], bn_col).then_inc(params_in, 16)
            sp.dma_start(alphas[:, :], to_all_partitions(alpha)).then_inc(params_in, 16)
            for n, w in enumerate((wq, wk, wv)):
                sp.dma_start(wqkv[:, :, n, :], w.rearrange("(t p) o -> p t o", p=128)).then_inc(weights_in, 16)
            for d, w in enumerate((wd1, wd2, wd3)):
                sp.dma_start(wconv[0:3 * IC, d], w).then_inc(weights_in, 16)
            sp.dma_start(wout[:, :], wo).then_inc(weights_in, 16)
            sp.wait_ge(zeros_set, 1)
            for n in range(B * IC // 128):
                for at in (0, (HP - PAD) * WP):
                    sp.dma_start(v_bands[128 * n:128 * n + 128, at:at + PAD * WP], zeros).then_inc(pads_out, 16)
            sp.wait_ge(pads_out, PAD_DMAS * 16)

            def load_x(b, s, m):
                sp.wait_ge(qkv_done, b * NCH + s + 1)
                sp.dma_start(xbuf[:, m], x_rows[b, :, :, bass.ds(s * (R * W), R * W)]).then_inc(xa_in[m], 16)

            def load_windows(b, s, m, stored_same, stored_other):
                sp.wait_ge(v_out[m], stored_same * 16 + 16)
                sp.wait_ge(v_out[1 - m], stored_other * 16 + 16)
                sp.sem_inc(waited, 1)
                sp.wait_ge(conv_done, b * NCH + s + 1)
                for d in range(ND):
                    rows = bass.AP(
                        tensor=vpad.tensor,
                        offset=vpad.offset + b * (IC * HP * WP) + s * (R * WP) + (PAD - DIL[d]) * WP,
                        ap=[[HP * WP, IC], [DIL[d] * WP, 3], [1, R * WP]])
                    sp.dma_start(win[0:3 * IC, m, d * R * WP:(d + 1) * R * WP], rows).then_inc(win_in[m], 16)

            def rows_loads(b):
                for s in range(LAG):
                    load_x(b, s, s % 2)
                with sp.Fori(0, NH - LAG // 2) as i:
                    for m in (0, 1):
                        load_x(b, 2 * i + (m + LAG), m)
                        load_windows(b, 2 * i + m, m, b * NH + i + 2, b * NH + i + (1 + m))
                for s in range(NCH - LAG, NCH):
                    load_windows(b, s, s % 2, b * NH + min(s // 2 + 2, NH), b * NH + min((s + 1) // 2 + 1, NH))

            def proj_loads(k, target):
                with sp.Fori(0, NH) as i:
                    for m in (0, 1):
                        v = 2 * i + m
                        sp.wait_ge(zt_turned, k * NCH + v + 1)
                        pixels = bass.AP(
                            tensor=att.tensor, offset=att.offset + target * (W * H * NB) + v * (R * NB),
                            ap=[[H * NB, HALF], [HALF * H * NB, 2], [1, R * NB]])
                        sp.dma_start(win[0:HALF, m, 0:ZT].rearrange("p (f n) -> p f n", f=2), pixels).then_inc(zt_in[m], 16)
                        sp.wait_ge(z_added, (k * NCH + v) * 4 + 4)
                        sp.dma_start(xbuf[:, m], x_rows[target, :, :, bass.ds(v * (R * W), R * W)]).then_inc(xb_in[m], 16)

            def attended_stored(images):
                for m in (0, 1):
                    sp.wait_ge(att_out[m], images * (NH * G * 16) + 16)
                sp.sem_inc(waited, 1)

            with sp.Fori(0, LEAD) as b:
                rows_loads(b)
            with sp.Fori(0, B - LEAD) as k:
                sp.wait_ge(z_added, k * (4 * NCH) + 8)
                sp.sem_inc(waited, 1)
                sp.wait_ge(pr_done, k * (4 * NCH) + 1)
                sp.sem_inc(waited, 1)
                rows_loads(k + LEAD)
                sp.wait_ge(qkv_done, (k + LEAD + 1) * NCH + 2)
                sp.sem_inc(waited, 1)
                sp.wait_ge(conv_done, (k + LEAD + 1) * NCH + 2)
                sp.sem_inc(waited, 1)
                attended_stored(k + LEAD)
                proj_loads(k, (3 * k) % B)
            attended_stored(B)
            with sp.Fori(B - LEAD, B) as k:
                proj_loads(k, (3 * k) % B)

        @block.gpsimd
        def _(pool):
            for s, n in CREDIT.items():
                pool.sem_inc(s, n)
            pool.memset(zeros, 0.0).then_inc(zeros_set, 1)
            pool.wait_ge(zeros_set, 1)
            done = [0]

            def const(ins):
                done[0] += 1
                ins.then_inc(consts, 1)
                pool.wait_ge(consts, done[0])

            for t in (ident[:, :], quarter[:, :], win[96:128, :, :], wconv[96:128], qdiag[:, :, :, :],
                      vbuf[:, :, :]):
                const(pool.memset(t, 0.0))
            const(pool.affine_select(out=ident[:, :], in_=ident[:, :], compare_op=ALU.not_equal, fill=1.0,
                                     base=0, pattern=[[-1, 128]], channel_multiplier=1))
            for g in range(G):
                const(pool.memset(quarter[IC * g:IC * g + IC, g:g + 1], 1.0))
            const(pool.memset(win[96:97, :, :], 1.0))
            for t in (tcol, tfirst):
                const(pool.memset(t[:, :, :, NB:NV], 1.0))
            const(pool.tensor_copy(signed_quarter[:, :], quarter[:, :]))
            assert done[0] == CONSTS

            def stage_qk(b, u, m):
                pool.wait_ge(s_done, (b * NCH + u) * 2 + 2)
                pool.sem_inc(waited, 1)
                pool.tensor_copy(kcol[:, m].rearrange("c (n p) -> c n p", n=NHB),
                                 k_img[:, bass.ds(u, 1), :].rearrange("c o (p n) -> c (o n) p", n=NHB)).then_inc(qk_staged, 1)
                pool.tensor_tensor(
                    qdiag[:, m].rearrange("c q (g p) -> c q g p", g=G),
                    q_img[:, bass.ds(u, 1), :].rearrange("c o (p q) -> c (o q) p", q=NQ).unsqueeze(2)
                    .to_broadcast([128, NQ, G, IC]),
                    signed_quarter[:, :].unsqueeze(1).unsqueeze(3).to_broadcast([128, NQ, G, IC]),
                    ALU.mult).then_inc(qk_staged, 1)

            def stage_t(b, u, m):
                pool.wait_ge(pv_done, b * NCH + u + 1)
                pool.sem_inc(waited, 1)
                pool.tensor_copy(tcol[:, m, :, 0:NB].rearrange("c h (d n) -> c h d n", d=ND),
                                 t_img[:, bass.ds(u, 1)].rearrange("c o d (h n) -> c (o h) d n", h=NHB)).then_inc(t_staged, 1)

            pool.wait_ge(setup_dve, SETUP_STEPS)
            with pool.Fori(0, B) as b:
                pool.wait_ge(qk_kept, (b + 1) * (2 * NCH))
                pool.wait_ge(conv_kept, (b + 1) * NCH + 2)
                stage_qk(b, 0, 0)
                stage_qk(b, 1, 1)
                with pool.Fori(0, NH - 1) as i:
                    for m in (0, 1):
                        stage_t(b, 2 * i + m, m)
                        stage_qk(b, 2 * i + (m + 2), m)
                for u in (NCH - 2, NCH - 1):
                    stage_t(b, u, u % 2)

        @block.tensor
        def _(pe):
            pe.wait_ge(setup_dve, SETUP_STEPS)
            pe.wait_ge(consts, CONSTS)

            def qkv(b, s, i, m):
                pe.wait_ge(xa_in[m], (b * NH + i + 1) * 16)
                pe.wait_ge(v_kept, b * NCH + s + 1)
                rows = xbuf[:, m].rearrange("p t (h w) -> p t h w", h=R)
                bank = qkv_ps[m]
                for n in range(2):
                    for t in range(KT):
                        for g in range(G):
                            pe.matmul(bank[IC * g:IC * g + IC, n * PX:(n + 1) * PX], wqkv[:, t, n, :],
                                      rows[:, t, :, WG * g:WG * g + WG], start=(t == 0), stop=(t == KT - 1))
                for t in range(KT):
                    for r in range(R):
                        mm = pe.matmul(bank[IC * r:IC * r + IC, 2 * PX:2 * PX + W], wqkv[:, t, 2, :],
                                       rows[:, t, r, :], start=(t == 0), stop=(t == KT - 1))
                mm.then_inc(qkv_done, 1)

            def conv(b, s, i, m):
                pe.wait_ge(win_in[m], (b * NH + i + 1) * (ND * 16))
                pe.wait_ge(conv_kept, b * NCH + s + 1)
                for d in range(ND):
                    for kw in range(3):
                        at = PAD + (kw - 1) * DIL[d]
                        for g in range(G):
                            mm = pe.matmul(conv_ps[m][IC * g:IC * g + IC, d * PX:(d + 1) * PX], wconv[:, d, kw, :],
                                           window[:, m, d, :, WG * g + at:WG * g + at + WG],
                                           start=(kw == 0), stop=(kw == 2))
                mm.then_inc(conv_done, 1)

            def rows_to_qkvt(b):
                pe.wait_ge(pa_kept, b * NCH + 1)
                pe.wait_ge(pt_kept, b * (2 * NCH) + 2)
                pe.wait_ge(tf_kept, b * NCH + 1)
                pe.wait_ge(o_kept, b * NCH + 1)
                for s in range(LAG):
                    qkv(b, s, s // 2, s % 2)
                with pe.Fori(0, NH - LAG // 2) as i:
                    for m in (0, 1):
                        qkv(b, 2 * i + (m + LAG), i + LAG // 2, m)
                        conv(b, 2 * i + m, i, m)
                for s in range(NCH - LAG, NCH):
                    conv(b, s, s // 2, s % 2)

            def scores(U, m):
                pe.wait_ge(qk_staged, (U + 1) * 2)
                for n, qs in enumerate((range(SQ), range(SQ, NQ))):
                    pe.wait_ge(exp_done, U * NQ + (SQ, NQ)[n])
                    for a, q in enumerate(qs):
                        mm = pe.matmul(s_ps[n][:, H * a:H * a + H], qdiag[:, m, q, :], kcol[:, m, :], start=True, stop=True)
                    mm.then_inc(s_done, 1)

            def regroup(U, m):
                pe.wait_ge(t_staged, U + 1)
                pe.wait_ge(tf_kept, U + 1)
                for g in range(G):
                    for h in range(NA):
                        mm = pe.matmul(rg_ps[IC * h:IC * h + IC, NB * g:NB * g + NB], ident[:, IC * g:IC * g + IC],
                                       tcol[:, m, h, 0:NB], start=True, stop=True)
                mm.then_inc(rg_done, 1)

            def turn_prob(U, m):
                pe.wait_ge(exp_done, U * NQ + (NQ + FIRST))
                pe.wait_ge(pa_kept, U + 1)
                for q in range(FIRST):
                    mm = pe.transpose(pt_ps[0][:, 128 * q:128 * q + 128], prob[:, m, q, 0:128], ident[:, :])
                mm.then_inc(pt_done, 1)
                pe.wait_ge(exp_done, U * NQ + 2 * NQ)
                pe.wait_ge(pt_kept, U * 2 + 2)
                pe.transpose(pt_ps[1][:, 0:128], prob[:, m, FIRST, 0:128], ident[:, :])
                for q in range(NQ):
                    for g in range(G):
                        mm = pe.matmul(pt_ps[1][IC * g:IC * g + IC, 128 + IC * q:128 + IC * q + IC],
                                       prob[:, m, q, 128:H], ident[:, IC * g:IC * g + IC], start=True, stop=True)
                mm.then_inc(pt_done, 1)

            def attend(U, m):
                pe.wait_ge(t_staged, U + 1)
                pe.wait_ge(tf_kept, U + 2)
                pe.wait_ge(pa_kept, U + 2)
                pe.wait_ge(pt_kept, U * 2 + 4)
                pe.wait_ge(o_kept, U + 1)
                for q in range(NQ):
                    for j in range(2):
                        for g in range(G):
                            mm = pe.matmul(pv_ps[IC * g:IC * g + IC, NV * q:NV * q + NV],
                                           probT[:, m, NQ * j + q, IC * g:IC * g + IC],
                                           tcol[:, m, NHB - 1, :] if j else tfirst[:, m, g, :],
                                           start=(j == 0), stop=(j == 1))
                mm.then_inc(pv_done, 1)

            def turn_z(V, k, i, m):
                pe.wait_ge(zt_in[m], (k * NH + i + 1) * 16)
                for n in range(2):
                    pe.wait_ge(z_added, V * 4 + (7 + n))
                    for r in range(2):
                        for f in range(2):
                            at = W * r + HALF * f
                            mm = pe.transpose(pr_ps[n][0:NB, at:at + HALF], zt[:, m, f, 2 * n + r, :], ident[0:HALF, 0:HALF])
                    mm.then_inc((z_turned, zt_turned)[n], 1)

            def project(V, n, m):
                for f in range(KT):
                    if n == 0:
                        pe.wait_ge(zc_kept, V * 2 + (f + 1))
                    else:
                        pe.wait_ge(z_added, V * 4 + (9 + f))
                    pe.matmul(pr_ps[f][:, 0:2 * W], wout[:, 128 * f:128 * f + 128],
                              zc[:, m, 2 * W * n:2 * W * n + 2 * W], start=True, stop=True).then_inc(pr_done, 1)

            def slot(b, u, i, m, k, first=False, last=False):
                U = b * NCH + u
                if k is not None:
                    V = k * NCH + u
                    turn_z(V, k, i, m)
                if not last:
                    scores(U + 1, 1 - m)
                regroup(U, m)
                if k is not None:
                    project(V, 0, m)
                turn_prob(U, m)
                if k is not None:
                    project(V, 1, m)
                if not first:
                    attend(U - 1, 1 - m)

            def columns(b, k=None):
                scores(b * NCH, 0)
                slot(b, 0, 0, 0, k, first=True)
                slot(b, 1, 0, 1, k)
                with pe.Fori(1, NH - 1) as i:
                    for m in (0, 1):
                        slot(b, 2 * i + m, i, m, k)
                slot(b, NCH - 2, NH - 1, 0, k)
                slot(b, NCH - 1, NH - 1, 1, k, last=True)
                attend(b * NCH + (NCH - 1), 1)

            with pe.Fori(0, LEAD) as b:
                rows_to_qkvt(b)
                columns(b)
            with pe.Fori(0, B - LEAD) as k:
                rows_to_qkvt(k + LEAD)
                columns(k + LEAD, k)
            with pe.Fori(B - LEAD, B) as k:
                with pe.Fori(0, NH) as i:
                    for m in (0, 1):
                        V = k * NCH + 2 * i + m
                        turn_z(V, k, i, m)
                        project(V, 0, m)
                        project(V, 1, m)

        @block.vector
        def _(dve):
            steps = [0]

            def step(ins):
                steps[0] += 1
                ins.then_inc(setup_dve, 1)
                dve.wait_ge(setup_dve, steps[0])

            dve.wait_ge(params_in, 48)
            step(dve.tensor_scalar(ptmp, var, EPS, None, ALU.add))
            step(dve.reciprocal(pinv, ptmp))
            dve.wait_ge(setup_root, 1)
            step(dve.tensor_tensor(pinv, proot, proot, ALU.mult))
            step(dve.tensor_tensor(pinv, pinv, ptmp, ALU.mult))
            step(dve.tensor_scalar(pinv, pinv, -0.5, 1.5, ALU.mult, ALU.add))
            step(dve.tensor_tensor(proot, proot, pinv, ALU.mult))
            step(dve.tensor_tensor(pscale, proot, gamma, ALU.mult))
            step(dve.tensor_tensor(pbias, mean, pscale, ALU.mult))
            step(dve.tensor_tensor(pbias, beta, pbias, ALU.subtract))
            step(dve.tensor_copy(colbias[:, :], pbias[:, NPR:NP]))
            step(dve.tensor_scalar(sign[:, :], alphas[:, :], 1.0, 2.0, ALU.is_le, ALU.mult))
            step(dve.tensor_scalar(sign[:, :], sign[:, :], -1.0, None, ALU.add))
            step(dve.tensor_scalar(unleak[:, :], alphas[:, :], -1.0, 1.0, ALU.mult, ALU.add))
            step(dve.tensor_tensor(colbias[:, 0:3], colbias[:, 0:3], sign[:, 0:3], ALU.mult))
            step(dve.tensor_tensor(leakbias[:, :], colbias[:, 0:3], alphas[:, 0:3], ALU.mult))
            dve.wait_ge(weights_in, 7 * 16)
            dve.wait_ge(consts, CONSTS)
            for t in range(KT):
                w = wqkv[:, t].rearrange("p n o -> p (n o)")
                step(dve.tensor_tensor(w, w, pscale[:, 0:3 * IC], ALU.mult))
            for n in range(3):
                step(dve.tensor_scalar(wqkv[:, :, n, :], wqkv[:, :, n, :], sign[:, n:n + 1], None, ALU.mult))
            step(dve.tensor_scalar(signed_quarter[:, :], signed_quarter[:, :], sign[:, 0:1], sign[:, 1:2], ALU.mult, ALU.mult))
            v_rows = wconv[0:3 * IC].rearrange("p d k o -> p (d k o)")
            step(dve.tensor_scalar(v_rows, v_rows, sign[0:3 * IC, 2:3], None, ALU.mult))
            for d in range(ND):
                cols = slice(3 * IC + d * IC, 3 * IC + (d + 1) * IC)
                for kw in range(3):
                    w = wconv[0:3 * IC, d, kw]
                    step(dve.tensor_tensor(w, w, pscale[0:3 * IC, cols], ALU.mult))
                step(dve.tensor_copy(wconv[3 * IC:3 * IC + 1, d, 0], pbias[3 * IC:3 * IC + 1, cols]))
            step(dve.tensor_tensor(wout[:, :], wout[:, :], pscale[0:NB, 3 * IC + NB:NPR], ALU.mult))
            assert steps[0] == SETUP_STEPS
            dve.wait_ge(pads_out, PAD_DMAS * 16)

            def keep_qkv(b, s, i, m):
                p = qkv_ps[m]
                dve.wait_ge(leak_ready, (b * NCH + s) * 3 + 3)
                for n, img in enumerate((q_img, k_img)):
                    dve.scalar_tensor_tensor(
                        out=img[:, :, bass.ds(s * R, R)],
                        in0=p[:, n * PX:(n + 1) * PX].rearrange("p (h w) -> p w h", h=R), scalar=colbias[:, n:n + 1],
                        in1=leak[:, m, n * PX:(n + 1) * PX].rearrange("p (h w) -> p w h", h=R),
                        op0=ALU.add, op1=ALU.max).then_inc(qk_kept, 1)
                dve.wait_ge(v_out[m], (b * NH + i) * 16 + 16)
                dve.scalar_tensor_tensor(
                    out=vbuf[:, m, PAD:PAD + W], in0=p[:, 2 * PX:3 * PX], scalar=colbias[:, 2:3],
                    in1=leak[:, m, 2 * PX:3 * PX], op0=ALU.add, op1=ALU.max).then_inc(v_kept, 1)

            def rows_to_qkv(b):
                with dve.Fori(0, NH) as i:
                    for m in (0, 1):
                        keep_qkv(b, 2 * i + m, i, m)

            def row_max(U, m):
                for n, (a, z) in enumerate(((0, SQ), (SQ, NQ))):
                    dve.wait_ge(s_done, U * 2 + (n + 5))
                    dve.tensor_reduce(nmax[:, m, a:z], s_ps[n][:, 0:H * (z - a)].rearrange("p (q j) -> p q j", j=H),
                                      AX_X, ALU.max, negate=True).then_inc(max_done, 1)

            def keep_probT(U, m):
                dve.wait_ge(pt_done, U * 2 + 2)
                dve.tensor_copy(probT[:, m, FIRST], pt_ps[1][:, 0:128]).then_inc(pt_kept, 1)
                dve.tensor_tensor(
                    probT[:, m, NQ:2 * NQ].rearrange("c q (g p) -> c q g p", g=G),
                    pt_ps[1][:, 128:128 + NQ * IC].rearrange("c (q p) -> c q p", q=NQ).unsqueeze(2).to_broadcast([128, NQ, G, IC]),
                    quarter[:, :].unsqueeze(1).unsqueeze(3).to_broadcast([128, NQ, G, IC]), ALU.mult).then_inc(pt_kept, 1)

            def normalise(b, U, i, m):
                dve.wait_ge(pv_done, U + 3)
                pv = pv_ps[:, 0:NQ * NV].rearrange("p (q n) -> p q n", n=NV)
                dve.reciprocal(rden[:, m], pv[:, :, NB]).then_inc(den_done, 1)
                dve.wait_ge(den_done, U + 1)
                dve.wait_ge(att_out[m], (b * NH + i) * (G * 16) + 16)
                dve.tensor_tensor(obuf[:, m].rearrange("p r q c -> p q r c"),
                                  pv[:, :, 0:NB].rearrange("p q (r c) -> p q r c", r=ND),
                                  rden[:, m].unsqueeze(2).unsqueeze(3).to_broadcast([128, NQ, ND, IC]),
                                  ALU.mult).then_inc(o_kept, 1)

            def residual(V, k, i, n, m):
                if n == 0:
                    dve.wait_ge(xb_in[m], (k * NH + i + 1) * 16)
                    dve.wait_ge(z_out[m], (k * NH + i) * 16 + 16)
                rows = slice(2 * W * n, 2 * W * n + 2 * W)
                for f in range(KT):
                    dve.wait_ge(pr_done, V * 4 + (2 * n + f + 2))
                    dve.scalar_tensor_tensor(out=zbuf[:, m, f, rows], in0=pr_ps[f][:, 0:2 * W],
                                             scalar=colbias[:, 3 + f:4 + f], in1=xbuf[:, m, f, rows],
                                             op0=ALU.add, op1=ALU.add).then_inc(z_added, 1)

            def prelu_out(V, m):
                dve.wait_ge(r_ready, V + 1)
                z = zbuf[:, m].rearrange("p t n -> p (t n)")
                dve.scalar_tensor_tensor(out=z, in0=rbuf[:, :], scalar=unleak[:, 3:4], in1=z,
                                         op0=ALU.mult, op1=ALU.add).then_inc(z_done, 1)

            def slot(b, u, i, m, k, first=False, last=False):
                U = b * NCH + u
                if not last:
                    row_max(U + 1, 1 - m)
                if k is not None:
                    if not first:
                        prelu_out(k * NCH + u - 1, 1 - m)
                    residual(k * NCH + u, k, i, 0, m)
                keep_probT(U, m)
                if k is not None:
                    residual(k * NCH + u, k, i, 1, m)
                if not first:
                    normalise(b, U - 1, i + (m - 1), 1 - m)

            def columns(b, k=None):
                row_max(b * NCH, 0)
                slot(b, 0, 0, 0, k, first=True)
                slot(b, 1, 0, 1, k)
                with dve.Fori(1, NH - 1) as i:
                    for m in (0, 1):
                        slot(b, 2 * i + m, i, m, k)
                slot(b, NCH - 2, NH - 1, 0, k)
                slot(b, NCH - 1, NH - 1, 1, k, last=True)
                normalise(b, b * NCH + (NCH - 1), NH - 1, 1)
                if k is not None:
                    prelu_out(k * NCH + (NCH - 1), 1)

            with dve.Fori(0, LEAD) as b:
                rows_to_qkv(b)
                columns(b)
            with dve.Fori(0, B - LEAD) as k:
                rows_to_qkv(k + LEAD)
                columns(k + LEAD, k)
            with dve.Fori(B - LEAD, B) as k:
                for m in (0, 1):
                    for n in range(2):
                        residual(k * NCH + m, k, 0, n, m)
                prelu_out(k * NCH, 0)
                with dve.Fori(0, NH - 1) as i:
                    for m in (0, 1):
                        for n in range(2):
                            residual(k * NCH + 2 * i + (m + 2), k, i + 1, n, m)
                        prelu_out(k * NCH + 2 * i + (m + 1), 1 - m)
                prelu_out(k * NCH + (NCH - 1), 1)

        @block.scalar
        def _(act):
            act.wait_ge(setup_dve, 2)
            act.activation(proot, pinv, ACT.Sqrt).then_inc(setup_root, 1)
            act.wait_ge(params_in, 48)
            act.wait_ge(setup_dve, SETUP_STEPS)
            act.wait_ge(consts, CONSTS)

            def leak_qkv(b, s, m):
                act.wait_ge(qkv_done, b * NCH + s + 3)
                act.wait_ge(v_kept, b * NCH + s + 1)
                for n in range(3):
                    act.activation(leak[:, m, n * PX:(n + 1) * PX], qkv_ps[m][:, n * PX:(n + 1) * PX], ACT.Identity,
                                   bias=leakbias[:, n:n + 1], scale=alphas[:, n:n + 1]).then_inc(leak_ready, 1)

            def store_v(b, s, m):
                act.wait_ge(v_kept, b * NCH + s + 3)
                rows = bass.AP(
                    tensor=vpad.tensor,
                    offset=vpad.offset + b * (IC * HP * WP) + s * (R * WP) + PAD * WP,
                    ap=[[WP, R], [HP * WP, IC], [1, WP]])
                act.dma_start(rows, vbuf[:, m]).then_inc(v_out[m], 16)

            def keep_conv(b, s, m):
                act.wait_ge(conv_done, b * NCH + s + 3)
                act.activation(t_img[:, :, :, bass.ds(s * R, R)],
                               conv_ps[m][:, 0:ND * PX].rearrange("p (d h w) -> p w d h", d=ND, h=R),
                               ACT.Relu).then_inc(conv_kept, 1)

            def rows_to_qkvt(b):
                leak_qkv(b, 0, 0)
                for s in range(1, LAG):
                    leak_qkv(b, s, s % 2)
                    store_v(b, s - 1, (s - 1) % 2)
                with act.Fori(0, NH - LAG // 2) as i:
                    for m in (0, 1):
                        leak_qkv(b, 2 * i + (m + LAG), m)
                        store_v(b, 2 * i + (m + LAG - 1), 1 - m)
                        keep_conv(b, 2 * i + m, m)
                store_v(b, NCH - 1, 1)
                for s in range(NCH - LAG, NCH):
                    keep_conv(b, s, s % 2)

            def keep_regrouped(U, m):
                act.wait_ge(rg_done, U + 1)
                act.activation(tfirst[:, m, :, 0:NB], rg_ps[:, 0:G * NB].rearrange("p (g n) -> p g n", g=G),
                               ACT.Copy).then_inc(tf_kept, 1)

            def keep_first_tiles(U, m):
                act.wait_ge(pt_done, U * 2 + 1)
                act.activation(probT[:, m, 0:FIRST].rearrange("p a i -> p (a i)"), pt_ps[0][:, :], ACT.Copy).then_inc(pa_kept, 1)

            def store_attended(b, u, m):
                act.wait_ge(o_kept, b * NCH + u + 2)
                for g in range(G):
                    rows = bass.AP(
                        tensor=att.tensor,
                        offset=att.offset + b * (W * H * IC) + u * (H * IC) + g * (WG * H * IC),
                        ap=[[NQ * IC, IC], [B * W * H * IC, ND], [1, NQ * IC]])
                    act.dma_start(rows, obuf[IC * g:IC * g + IC, m].rearrange("p r q c -> p r (q c)")).then_inc(att_out[m], 16)

            def store_out(k, v, m):
                act.wait_ge(z_done, k * NCH + v + 2)
                act.dma_start(out_rows[(3 * k) % B, :, :, bass.ds(v * (R * W), R * W)], zbuf[:, m]).then_inc(z_out[m], 16)

            def exponentials(U, m, between=None):
                for q in range(NQ):
                    if q in (0, SQ):
                        act.wait_ge(max_done, U * 2 + (1 if q == 0 else 2))
                    a, n = (q, 0) if q < SQ else (q - SQ, 1)
                    act.activation(prob[:, m, q], s_ps[n][:, H * a:H * a + H], ACT.Exp,
                                   bias=nmax[:, m, q:q + 1]).then_inc(exp_done, 1)
                    if q == SQ - 1 and between is not None:
                        between()

            def keep_zc(V, m):
                for n in range(2):
                    act.wait_ge((z_turned, zt_turned)[n], V + (1, 3)[n])
                    act.activation(zc[:, m, 2 * W * n:2 * W * n + 2 * W], pr_ps[n][0:NB, 0:2 * W], ACT.Copy).then_inc(zc_kept, 1)

            def negative_part(V, m):
                act.wait_ge(z_added, V * 4 + 12)
                act.wait_ge(z_done, V + 1)
                act.activation(rbuf[:, :], zbuf[:, m].rearrange("p t n -> p (t n)"), ACT.Relu, scale=-1.0).then_inc(r_ready, 1)

            def slot(b, u, m, k, first=False, second=False, last=False):
                U = b * NCH + u
                if k is not None:
                    keep_zc(k * NCH + u, m)
                    if not first:
                        negative_part(k * NCH + u - 1, 1 - m)
                keep_regrouped(U, m)
                if last:
                    keep_first_tiles(U, m)
                else:
                    exponentials(U + 1, 1 - m, lambda: keep_first_tiles(U, m))
                if not first and not second:
                    store_attended(b, u - 2, m)
                if k is not None and not first:
                    store_out(k, u - 1, 1 - m)

            def columns(b, k=None):
                exponentials(b * NCH, 0)
                slot(b, 0, 0, k, first=True)
                slot(b, 1, 1, k, second=True)
                with act.Fori(1, NH - 1) as i:
                    for m in (0, 1):
                        slot(b, 2 * i + m, m, k)
                slot(b, NCH - 2, 0, k)
                slot(b, NCH - 1, 1, k, last=True)
                store_attended(b, NCH - 2, 0)
                store_attended(b, NCH - 1, 1)
                if k is not None:
                    negative_part(k * NCH + (NCH - 1), 1)
                    store_out(k, NCH - 1, 1)

            with act.Fori(0, LEAD) as b:
                rows_to_qkvt(b)
                columns(b)
            with act.Fori(0, B - LEAD) as k:
                rows_to_qkvt(k + LEAD)
                columns(k + LEAD, k)
            with act.Fori(B - LEAD, B) as k:
                keep_zc(k * NCH, 0)
                with act.Fori(0, NH - 1) as i:
                    for m in (0, 1):
                        keep_zc(k * NCH + 2 * i + (m + 1), 1 - m)
                        negative_part(k * NCH + 2 * i + m, m)
                        store_out(k, 2 * i + m, m)
                keep_zc(k * NCH + (NCH - 1), 1)
                for u in (NCH - 2, NCH - 1):
                    negative_part(k * NCH + u, u % 2)
                    store_out(k, u, u % 2)
            for m in (0, 1):
                act.wait_ge(z_out[m], B * NH * 16 + 16)
                act.wait_ge(v_out[m], B * NH * 16 + 16)
                act.wait_ge(att_out[m], B * NH * G * 16 + 16)


_BN = ("gamma", "beta", "mean", "var")


def kernel(**inputs):
    import concourse.bacc as bacc
    from concourse.bass_utils import run_bass_kernel_spmd

    p = {n[len("L0_conv_"):]: np.asarray(a) for n, a in inputs.items() if n != "x"}
    convs = ("d1", "d2", "d3")
    row = np.stack([np.concatenate([p[f"{n}_{s}"] for n in ("q", "k", "v") + convs + ("o",)]) for s in _BN])
    col = np.stack([np.stack([np.tile(p[f"{n}_{s}"], G) for n in ("q", "k", "v")]
                             + list(p[f"o_{s}"].reshape(KT, 128)), axis=-1) for s in _BN], axis=1)
    arrays = {
        "x": np.asarray(inputs["x"]),
        "wq": p["q_w"].T, "wk": p["k_w"].T, "wv": p["v_w"].T,
        **{f"w{n}": p[f"{n}_w"].transpose(1, 2, 3, 0).reshape(3 * IC, 3, IC) for n in convs},
        "wo": p["o_w"].T,
        "bn_row": row, "bn_col": col,
        "alpha": np.concatenate([p[f"{n}_alpha"] for n in ("q", "k", "v", "o")]),
    }
    arrays = {n: np.ascontiguousarray(a) for n, a in arrays.items()}
    nc = bacc.Bacc("TRN2", target_bir_lowering=False, num_devices=1)
    aps = [nc.dram_tensor(n, list(a.shape), mybir.dt.from_np(a.dtype), kind="ExternalInput").ap() for n, a in arrays.items()]
    out = nc.dram_tensor("out", [B, C, H, W], F32, kind="ExternalOutput").ap()
    build(nc, *aps, out)
    r = run_bass_kernel_spmd(nc, [arrays], core_ids=[0])
    return r.results[0]["out"]
```

```python
from contextlib import ExitStack

import numpy as np

import concourse.bass as bass
from concourse import mybir

F32 = mybir.dt.float32
ALU = mybir.AluOpType
ACT = mybir.ActivationFunctionType
AX_X = mybir.AxisListType.X

B, C, H, W = 8, 256, 160, 160
IC = 32
KT = C // 128
G = 4
WG = W // G
ND = 3
DIL = (1, 3, 5)
PAD = max(DIL)
HP, WP = H + 2 * PAD, W + 2 * PAD
R = 4
NCH = H // R
PX = R * WG
NQ = H // IC
NHB = H // IC
LAG = 6
NA = 128 // IC
NB = ND * IC
NV = NB + 1
HALF = W // 2
LEAD = 3
EPS = 1e-5
NPC = 2 * KT + 1
NPR = 3 * IC + NB + C
NH = NCH // 2
RING = 4
assert NCH % RING == 0 and NCH == WG and NCH % 2 == 0 and NHB == NA + 1 == NQ and R * WG == W


def build(nc, x, wq, wk, wv, wd1, wd2, wd3, wo, bn_row, bn_col, alpha, out):
    vpad = nc.dram_tensor("v_padded", [B, IC, HP, WP], F32, kind="Internal").ap()
    att = nc.dram_tensor("attended", [ND * B * W, H, IC], F32, kind="Internal").ap()

    x_rows = x.rearrange("b (t p) h w -> b p t (h w)", p=128)
    out_rows = out.rearrange("b (t p) h w -> b p t (h w)", p=128)
    v_bands = vpad.rearrange("b c h w -> (b c) (h w)")

    def to_all_partitions(a):
        return bass.AP(tensor=a.tensor, offset=a.offset, ap=[[0, 128]] + list(a.ap))

    with ExitStack() as ctx:
        def sb(name, shape):
            return ctx.enter_context(nc.sbuf_tensor(name, shape, F32))

        def sem(name):
            return ctx.enter_context(nc.semaphore(name))

        q_img = sb("q_img", [128, WG, H])
        k_img = sb("k_img", [128, WG, H])
        t_img = sb("t_img", [128, WG, ND, H])
        xbuf = sb("xbuf", [128, 2, KT, R * W])
        zbuf = sb("zbuf", [128, 2, KT, R * W])
        rbuf = sb("rbuf", [128, KT * R * W])
        win = sb("win", [128, 2, ND * R * WP])
        vbuf = sb("vbuf", [128, 2, WP])
        qdiag = sb("qdiag", [128, 2, NQ, 128])
        kcol = sb("kcol", [128, 2, H])
        tcol = sb("tcol", [128, 2, NHB, NV])
        tfirst = sb("tfirst", [128, 2, G, NV])
        prob = sb("prob", [128, 2, NQ, H])
        probT = sb("probT", [128, 2, 2 * NQ, 128])
        obuf = sb("obuf", [128, 2, ND, NQ, IC])
        wqkv = sb("wqkv", [128, KT, 3, IC])
        wconv = sb("wconv", [128, ND, 3, IC])
        wout = sb("wout", [NB, C])
        ident = sb("ident", [128, 128])
        signed_quarter = sb("signed_quarter", [128, G])
        nmax = sb("nmax", [128, 2, NQ])
        rden = sb("rden", [128, 2, NQ])
        alphas = sb("alphas", [128, 4])
        colbias = sb("colbias", [128, NPC])
        sign = sb("sign", [128, 4])
        leakbias = sb("leakbias", [128, 3])
        unleak = sb("unleak", [128, 4])

        leak = prob[:, :, 0:3].rearrange("p m n j -> p m (n j)")
        window = win[:, :, :].rearrange("p m (d r w) -> p m d r w", d=ND, r=R)
        ZT = 2 * R * NB
        zt = win[0:HALF, :, 0:ZT].rearrange("p m (f r j) -> p m f r j", f=2, r=R)
        zc = win[0:NB, :, ZT:ZT + R * W]
        def carve(img, parts, at, count, n):
            return img[0:parts].rearrange("p a n -> p (a n)")[:, at:at + count * n].rearrange("p (m n) -> p m n", m=count)

        t_flat = t_img[:, :, :, :].rearrange("p w d h -> p w (d h)")
        CHUNK = KT * R * W
        ring_x = carve(t_flat, 128, 0, RING, CHUNK)
        ring_z = carve(t_flat, 128, RING * CHUNK, RING, CHUNK)
        ring_r = carve(t_flat, 128, 2 * RING * CHUNK, 2, CHUNK)
        ring_zt = carve(q_img, HALF, 0, RING, ZT)
        ring_zc = carve(k_img, NB, 0, 2, R * W)
        NP = NPR + NPC
        scratch = t_img[:, :, :, :].rearrange("p w d h -> p (w d h)")
        prm = scratch[:, 0:4 * NP].rearrange("p (k n) -> p k n", k=4)
        gamma, beta, mean, var = (prm[:, n, :] for n in range(4))
        pinv, proot, ptmp, pscale, pbias = (
            scratch[:, (4 + n) * NP:(5 + n) * NP] for n in range(5))
        zeros = k_img[:, :, :].rearrange("p w h -> p (w h)")[:, 0:PAD * WP]

        ps = [ctx.enter_context(nc.psum_tensor(f"ps{n}", [128, 512], F32)) for n in range(8)]
        qkv_ps = [ps[2], ps[3]]
        conv_ps = [ps[4], ps[5]]
        s_ps = [ps[0], ps[1]]
        pt_ps = [ps[2], ps[3]]
        pv_ps = ps[5]
        pr_ps = [ps[6], ps[7]]
        SQ = 3

        params_in = sem("params_in")
        weights_in = sem("weights_in")
        setup_dve = sem("setup_dve")
        setup_root = sem("setup_root")
        consts = sem("consts")
        zeros_set = sem("zeros_set")
        waited = sem("waited")
        pads_out = sem("pads_out")
        xa_in = [sem(f"xa_in{m}") for m in (0, 1)]
        qkv_done = sem("qkv_done")
        leak_ready = sem("leak_ready")
        qk_kept = sem("qk_kept")
        v_kept = sem("v_kept")
        v_out = [sem(f"v_out{m}") for m in (0, 1)]
        win_in = [sem(f"win_in{m}") for m in (0, 1)]
        conv_done = sem("conv_done")
        conv_kept = sem("conv_kept")
        qk_staged = sem("qk_staged")
        t_staged = sem("t_staged")
        s_done = sem("s_done")
        max_done = sem("max_done")
        exp_done = sem("exp_done")
        tf_in = [sem(f"tf_in{m}") for m in (0, 1)]
        pt_done = sem("pt_done")
        pa_kept = sem("pa_kept")
        pt_kept = sem("pt_kept")
        pv_done = sem("pv_done")
        den_done = sem("den_done")
        o_kept = sem("o_kept")
        att_out = [sem(f"att_out{m}") for m in (0, 1)]
        xb_in = [sem(f"xb_in{m}") for m in (0, 1)]
        zt_in = [sem(f"zt_in{m}") for m in (0, 1)]
        z_turned = sem("z_turned")
        zt_turned = sem("zt_turned")
        zc_kept = sem("zc_kept")
        pr_done = sem("pr_done")
        z_added = sem("z_added")
        r_ready = sem("r_ready")
        z_done = sem("z_done")
        z_out = [sem(f"z_out{m}") for m in (0, 1)]

        last_x_in = [sem(f"last_x_in{m}") for m in range(RING)]
        last_zt_in = [sem(f"last_zt_in{m}") for m in range(RING)]
        last_turned = sem("last_turned")
        last_zc_kept = sem("last_zc_kept")
        last_pr_done = sem("last_pr_done")
        last_added = sem("last_added")
        last_r_ready = sem("last_r_ready")
        last_z_done = sem("last_z_done")
        last_z_out = [sem(f"last_z_out{m}") for m in range(RING)]

        PAD_DMAS = 2 * (B * IC // 128)
        CONSTS = 10 + G
        SETUP_STEPS = 15 + KT + 5 + 4 * ND + 1
        FIRST = NQ - 1
        CREDIT = {tf_in[0]: 16, tf_in[1]: 16, last_turned: 2 * RING, last_added: 4 * RING, last_z_done: 2, **{z: 16 for z in last_z_out},
                  qkv_done: 2, conv_done: 2, zt_turned: 2, s_done: 4, pv_done: 2, v_kept: 2, conv_kept: 2,
                  exp_done: NQ, pa_kept: 1, pt_kept: 2, o_kept: 1, z_added: 8, z_done: 1, pr_done: 1,
                  v_out[0]: 16, v_out[1]: 16, att_out[0]: 16, att_out[1]: 16, z_out[0]: 16, z_out[1]: 16}

        block = ctx.enter_context(nc.Block())

        @block.sync
        def _(sp):
            sp.dma_start(prm[:, :, 0:NPR], to_all_partitions(bn_row)).then_inc(params_in, 16)
            sp.dma_start(prm[:, :, NPR:NP], bn_col).then_inc(params_in, 16)
            sp.dma_start(alphas[:, :], to_all_partitions(alpha)).then_inc(params_in, 16)
            for n, w in enumerate((wq, wk, wv)):
                sp.dma_start(wqkv[:, :, n, :], w.rearrange("(t p) o -> p t o", p=128)).then_inc(weights_in, 16)
            for d, w in enumerate((wd1, wd2, wd3)):
                sp.dma_start(wconv[0:3 * IC, d], w).then_inc(weights_in, 16)
            sp.dma_start(wout[:, :], wo).then_inc(weights_in, 16)
            sp.wait_ge(zeros_set, 1)
            for n in range(B * IC // 128):
                for at in (0, (HP - PAD) * WP):
                    sp.dma_start(v_bands[128 * n:128 * n + 128, at:at + PAD * WP], zeros).then_inc(pads_out, 16)
            sp.wait_ge(pads_out, PAD_DMAS * 16)

            def load_x(b, s, m):
                sp.wait_ge(qkv_done, b * NCH + s + 1)
                sp.dma_start(xbuf[:, m], x_rows[b, :, :, bass.ds(s * (R * W), R * W)]).then_inc(xa_in[m], 16)

            def load_windows(b, s, m, stored_same, stored_other):
                sp.wait_ge(v_out[m], stored_same * 16 + 16)
                sp.wait_ge(v_out[1 - m], stored_other * 16 + 16)
                sp.sem_inc(waited, 1)
                sp.wait_ge(conv_done, b * NCH + s + 1)
                for d in range(ND):
                    rows = bass.AP(
                        tensor=vpad.tensor,
                        offset=vpad.offset + b * (IC * HP * WP) + s * (R * WP) + (PAD - DIL[d]) * WP,
                        ap=[[HP * WP, IC], [DIL[d] * WP, 3], [1, R * WP]])
                    sp.dma_start(win[0:3 * IC, m, d * R * WP:(d + 1) * R * WP], rows).then_inc(win_in[m], 16)

            def rows_loads(b):
                for s in range(LAG):
                    load_x(b, s, s % 2)
                with sp.Fori(0, NH - LAG // 2) as i:
                    for m in (0, 1):
                        load_x(b, 2 * i + (m + LAG), m)
                        load_windows(b, 2 * i + m, m, b * NH + i + 2, b * NH + i + (1 + m))
                for s in range(NCH - LAG, NCH):
                    load_windows(b, s, s % 2, b * NH + min(s // 2 + 2, NH), b * NH + min((s + 1) // 2 + 1, NH))

            def regroup(b, u, m):
                sp.wait_ge(t_staged, (b * NCH + u) * 2 + 1)
                sp.sem_inc(waited, 1)
                sp.wait_ge(pv_done, b * NCH + u + 1)
                for g in range(G):
                    sp.dma_start(tfirst[:, m, g, 0:NB],
                                 tcol[IC * g:IC * g + IC, m, 0:NA, 0:NB]).then_inc(tf_in[m], 16)

            def load_for_proj(k, v, m):
                target = (3 * k) % B
                sp.wait_ge(zt_turned, k * NCH + v + 1)
                pixels = bass.AP(
                    tensor=att.tensor, offset=att.offset + target * (W * H * NB) + v * (R * NB),
                    ap=[[H * NB, HALF], [HALF * H * NB, 2], [1, R * NB]])
                sp.dma_start(win[0:HALF, m, 0:ZT].rearrange("p (f n) -> p f n", f=2), pixels).then_inc(zt_in[m], 16)
                sp.wait_ge(z_added, (k * NCH + v) * 4 + 4)
                sp.dma_start(xbuf[:, m], x_rows[target, :, :, bass.ds(v * (R * W), R * W)]).then_inc(xb_in[m], 16)

            def columns(b, k=None):
                if k is not None:
                    for m in (0, 1):
                        load_for_proj(k, m, m)
                with sp.Fori(0, NH - 1) as i:
                    for m in (0, 1):
                        regroup(b, 2 * i + m, m)
                        if k is not None:
                            load_for_proj(k, 2 * i + (m + 2), m)
                for m in (0, 1):
                    regroup(b, NCH - 2 + m, m)

            def attended_stored(images):
                for m in (0, 1):
                    sp.wait_ge(att_out[m], images * (NH * ND * 16) + 16)
                sp.sem_inc(waited, 1)

            with sp.Fori(0, LEAD) as b:
                rows_loads(b)
                columns(b)
            with sp.Fori(0, B - LEAD) as k:
                sp.wait_ge(z_added, k * (4 * NCH) + 8)
                sp.sem_inc(waited, 1)
                sp.wait_ge(pr_done, k * (4 * NCH) + 1)
                sp.sem_inc(waited, 1)
                rows_loads(k + LEAD)
                sp.wait_ge(qkv_done, (k + LEAD + 1) * NCH + 2)
                sp.sem_inc(waited, 1)
                sp.wait_ge(conv_done, (k + LEAD + 1) * NCH + 2)
                sp.sem_inc(waited, 1)
                attended_stored(k + LEAD)
                columns(k + LEAD, k)
            attended_stored(B)
            sp.wait_ge(t_staged, B * NCH * 2)
            with sp.Fori(0, LEAD) as n:
                with sp.Fori(0, NCH // RING) as i:
                    for m in range(RING):
                        T = n * NCH + RING * i + m
                        target = (3 * n + 3 * (B - LEAD)) % B
                        sp.wait_ge(last_turned, T * 2 + 2)
                        pixels = bass.AP(
                            tensor=att.tensor, offset=att.offset + target * (W * H * NB) + (RING * i + m) * (R * NB),
                            ap=[[H * NB, HALF], [HALF * H * NB, 2], [1, R * NB]])
                        sp.dma_start(ring_zt[:, m].rearrange("p (f n) -> p f n", f=2), pixels).then_inc(last_zt_in[m], 16)
                        sp.wait_ge(last_added, T * 4 + 4)
                        sp.dma_start(ring_x[:, m].rearrange("p (t n) -> p t n", t=KT),
                                     x_rows[target, :, :, bass.ds((RING * i + m) * (R * W), R * W)]).then_inc(last_x_in[m], 16)

        @block.gpsimd
        def _(pool):
            for s, n in CREDIT.items():
                pool.sem_inc(s, n)
            pool.memset(zeros, 0.0).then_inc(zeros_set, 1)
            pool.wait_ge(zeros_set, 1)
            done = [0]

            def const(ins):
                done[0] += 1
                ins.then_inc(consts, 1)
                pool.wait_ge(consts, done[0])

            for t in (ident[:, :], signed_quarter[:, :], win[96:128, :, :], wconv[96:128], vbuf[:, :, :],
                      probT[:, :, NQ:2 * NQ]):
                const(pool.memset(t, 0.0))
            const(pool.affine_select(out=ident[:, :], in_=ident[:, :], compare_op=ALU.not_equal, fill=1.0,
                                     base=0, pattern=[[-1, 128]], channel_multiplier=1))
            for g in range(G):
                const(pool.memset(signed_quarter[IC * g:IC * g + IC, g:g + 1], 1.0))
            const(pool.memset(win[96:97, :, :], 1.0))
            for t in (tcol, tfirst):
                const(pool.memset(t[:, :, :, NB:NV], 1.0))
            assert done[0] == CONSTS

            def stage_qk(b, u, m):
                pool.wait_ge(s_done, (b * NCH + u) * 2 + 2)
                pool.sem_inc(waited, 1)
                keys = k_img[:, bass.ds(u, 1), :].rearrange("c o (p n) -> c (o p) n", n=NHB)
                pool.tensor_copy(kcol[:, m, 0:NA * IC].rearrange("c (p n) -> c p n", n=NA), keys[:, :, 0:NA]).then_inc(qk_staged, 1)
                pool.tensor_copy(kcol[:, m, NA * IC:].unsqueeze(2), keys[:, :, NA:NHB]).then_inc(qk_staged, 1)
                pool.tensor_tensor(
                    qdiag[:, m].rearrange("c q (g p) -> c q g p", g=G),
                    q_img[:, bass.ds(u, 1), :].rearrange("c o (p q) -> c (o q) p", q=NQ).unsqueeze(2)
                    .to_broadcast([128, NQ, G, IC]),
                    signed_quarter[:, :].unsqueeze(1).unsqueeze(3).to_broadcast([128, NQ, G, IC]),
                    ALU.mult).then_inc(qk_staged, 1)

            def stage_t(b, u, i, m):
                column = t_img[:, bass.ds(u, 1)].rearrange("c o d (h n) -> c (o h) d n", h=NHB)
                staged = tcol[:, m, :, 0:NB].rearrange("c h (d n) -> c h d n", d=ND)
                pool.wait_ge(tf_in[m], (b * NH + i) * (G * 16) + 16)
                pool.sem_inc(waited, 1)
                pool.tensor_copy(staged[:, 0:NA], column[:, 0:NA]).then_inc(t_staged, 1)
                pool.wait_ge(pv_done, b * NCH + u + 1)
                pool.sem_inc(waited, 1)
                pool.tensor_copy(staged[:, NA:NHB], column[:, NA:NHB]).then_inc(t_staged, 1)

            pool.wait_ge(setup_dve, SETUP_STEPS)
            with pool.Fori(0, B) as b:
                pool.wait_ge(qk_kept, (b + 1) * (2 * NCH))
                pool.wait_ge(conv_kept, (b + 1) * NCH + 2)
                stage_qk(b, 0, 0)
                stage_qk(b, 1, 1)
                with pool.Fori(0, NH - 1) as i:
                    for m in (0, 1):
                        stage_qk(b, 2 * i + (m + 2), m)
                        stage_t(b, 2 * i + m, i, m)
                for u in (NCH - 2, NCH - 1):
                    stage_t(b, u, NH - 1, u % 2)

        @block.tensor
        def _(pe):
            pe.wait_ge(setup_dve, SETUP_STEPS)
            pe.wait_ge(consts, CONSTS)

            def qkv(b, s, i, m):
                pe.wait_ge(xa_in[m], (b * NH + i + 1) * 16)
                pe.wait_ge(v_kept, b * NCH + s + 1)
                rows = xbuf[:, m].rearrange("p t (h w) -> p t h w", h=R)
                bank = qkv_ps[m]
                for n in range(2):
                    for t in range(KT):
                        for g in range(G):
                            pe.matmul(bank[IC * g:IC * g + IC, n * PX:(n + 1) * PX], wqkv[:, t, n, :],
                                      rows[:, t, :, WG * g:WG * g + WG], start=(t == 0), stop=(t == KT - 1))
                for t in range(KT):
                    for r in range(R):
                        mm = pe.matmul(bank[IC * r:IC * r + IC, 2 * PX:2 * PX + W], wqkv[:, t, 2, :],
                                       rows[:, t, r, :], start=(t == 0), stop=(t == KT - 1))
                mm.then_inc(qkv_done, 1)

            def conv(b, s, i, m):
                pe.wait_ge(win_in[m], (b * NH + i + 1) * (ND * 16))
                pe.wait_ge(conv_kept, b * NCH + s + 1)
                for d in range(ND):
                    for kw in range(3):
                        at = PAD + (kw - 1) * DIL[d]
                        for g in range(G):
                            mm = pe.matmul(conv_ps[m][IC * g:IC * g + IC, d * PX:(d + 1) * PX], wconv[:, d, kw, :],
                                           window[:, m, d, :, WG * g + at:WG * g + at + WG],
                                           start=(kw == 0), stop=(kw == 2))
                mm.then_inc(conv_done, 1)

            def rows_to_qkvt(b):
                pe.wait_ge(pa_kept, b * NCH + 1)
                pe.wait_ge(pt_kept, b * (2 * NCH) + 2)
                pe.wait_ge(o_kept, b * NCH + 1)
                for s in range(LAG):
                    qkv(b, s, s // 2, s % 2)
                with pe.Fori(0, NH - LAG // 2) as i:
                    for m in (0, 1):
                        qkv(b, 2 * i + (m + LAG), i + LAG // 2, m)
                        conv(b, 2 * i + m, i, m)
                for s in range(NCH - LAG, NCH):
                    conv(b, s, s // 2, s % 2)

            def scores(U, m):
                pe.wait_ge(qk_staged, (U + 1) * 3)
                for n, qs in enumerate((range(SQ), range(SQ, NQ))):
                    pe.wait_ge(exp_done, U * NQ + (SQ, NQ)[n])
                    for a, q in enumerate(qs):
                        mm = pe.matmul(s_ps[n][:, H * a:H * a + H], qdiag[:, m, q, :], kcol[:, m, :], start=True, stop=True)
                    mm.then_inc(s_done, 1)

            def turn_prob(U, m):
                pe.wait_ge(exp_done, U * NQ + (NQ + FIRST))
                pe.wait_ge(pa_kept, U + 1)
                for q in range(FIRST):
                    mm = pe.transpose(pt_ps[0][:, 128 * q:128 * q + 128], prob[:, m, q, 0:128], ident[:, :])
                mm.then_inc(pt_done, 1)
                pe.wait_ge(exp_done, U * NQ + 2 * NQ)
                pe.wait_ge(pt_kept, U * 2 + 2)
                pe.transpose(pt_ps[1][:, 0:128], prob[:, m, FIRST, 0:128], ident[:, :]).then_inc(pt_done, 1)

            def attend(b, U, i, m):
                pe.wait_ge(t_staged, U * 2 + 2)
                pe.wait_ge(tf_in[m], (b * NH + i + 1) * (G * 16) + 16)
                pe.wait_ge(pa_kept, U + 2)
                pe.wait_ge(pt_kept, U * 2 + 4)
                pe.wait_ge(o_kept, U + 1)
                for q in range(NQ):
                    cols = slice(NV * q, NV * q + NV)
                    pe.matmul(pv_ps[:, cols], probT[:, m, NQ + q, :], tcol[:, m, NHB - 1, :], start=True, stop=False)
                    for g in range(G):
                        mm = pe.matmul(pv_ps[IC * g:IC * g + IC, cols], probT[:, m, q, IC * g:IC * g + IC],
                                       tfirst[:, m, g, :], start=False, stop=True)
                mm.then_inc(pv_done, 1)

            def turn_z(V, k, i, m):
                pe.wait_ge(zt_in[m], (k * NH + i + 1) * 16)
                for n in range(2):
                    pe.wait_ge(z_added, V * 4 + (7 + n))
                    for r in range(2):
                        for f in range(2):
                            at = W * r + HALF * f
                            mm = pe.transpose(pr_ps[n][0:NB, at:at + HALF], zt[:, m, f, 2 * n + r, :], ident[0:HALF, 0:HALF])
                    mm.then_inc((z_turned, zt_turned)[n], 1)

            def project(V, n, m):
                for f in range(KT):
                    if n == 0:
                        pe.wait_ge(zc_kept, V * 2 + (f + 1))
                    else:
                        pe.wait_ge(z_added, V * 4 + (9 + f))
                    pe.matmul(pr_ps[f][:, 0:2 * W], wout[:, 128 * f:128 * f + 128],
                              zc[:, m, 2 * W * n:2 * W * n + 2 * W], start=True, stop=True).then_inc(pr_done, 1)

            def slot(b, u, i, m, k, first=False, last=False):
                U = b * NCH + u
                if k is not None:
                    V = k * NCH + u
                    turn_z(V, k, i, m)
                if not last:
                    scores(U + 1, 1 - m)
                if k is not None:
                    project(V, 0, m)
                turn_prob(U, m)
                if k is not None:
                    project(V, 1, m)
                if not first:
                    attend(b, U - 1, i + (m - 1), 1 - m)

            def columns(b, k=None):
                scores(b * NCH, 0)
                slot(b, 0, 0, 0, k, first=True)
                slot(b, 1, 0, 1, k)
                with pe.Fori(1, NH - 1) as i:
                    for m in (0, 1):
                        slot(b, 2 * i + m, i, m, k)
                slot(b, NCH - 2, NH - 1, 0, k)
                slot(b, NCH - 1, NH - 1, 1, k, last=True)
                attend(b, b * NCH + (NCH - 1), NH - 1, 1)

            with pe.Fori(0, LEAD) as b:
                rows_to_qkvt(b)
                columns(b)
            with pe.Fori(0, B - LEAD) as k:
                rows_to_qkvt(k + LEAD)
                columns(k + LEAD, k)
            pe.wait_ge(o_kept, B * NCH + 1)
            pe.wait_ge(pt_kept, B * NCH * 2 + 2)
            pe.wait_ge(z_added, (B - LEAD) * (4 * NCH) + 8)
            with pe.Fori(0, LEAD * NCH // RING) as i:
                for m in range(RING):
                    T = RING * i + m
                    pe.wait_ge(last_zt_in[m], i * 16 + 16)
                    zts = ring_zt[:, m].rearrange("p (f r j) -> p f r j", f=2, r=R)
                    for n in range(2):
                        for r in range(2):
                            for f in range(2):
                                at = W * r + HALF * f
                                mm = pe.transpose(ps[n][0:NB, at:at + HALF], zts[:, f, 2 * n + r, :], ident[0:HALF, 0:HALF])
                        mm.then_inc(last_turned, 1)
                    for n in range(2):
                        pe.wait_ge(last_zc_kept, T * 2 + (n + 1))
                        for f in range(KT):
                            pe.wait_ge(last_added, T * 4 + (4 * RING - 4 + 2 * n + f + 1))
                            pe.matmul(ps[4 + 2 * n + f][:, 0:2 * W], wout[:, 128 * f:128 * f + 128],
                                      ring_zc[:, m % 2, 2 * W * n:2 * W * n + 2 * W], start=True, stop=True).then_inc(last_pr_done, 1)

        @block.vector
        def _(dve):
            steps = [0]

            def step(ins):
                steps[0] += 1
                ins.then_inc(setup_dve, 1)
                dve.wait_ge(setup_dve, steps[0])

            dve.wait_ge(params_in, 48)
            step(dve.tensor_scalar(ptmp, var, EPS, None, ALU.add))
            step(dve.reciprocal(pinv, ptmp))
            dve.wait_ge(setup_root, 1)
            step(dve.tensor_tensor(pinv, proot, proot, ALU.mult))
            step(dve.tensor_tensor(pinv, pinv, ptmp, ALU.mult))
            step(dve.tensor_scalar(pinv, pinv, -0.5, 1.5, ALU.mult, ALU.add))
            step(dve.tensor_tensor(proot, proot, pinv, ALU.mult))
            step(dve.tensor_tensor(pscale, proot, gamma, ALU.mult))
            step(dve.tensor_tensor(pbias, mean, pscale, ALU.mult))
            step(dve.tensor_tensor(pbias, beta, pbias, ALU.subtract))
            step(dve.tensor_copy(colbias[:, :], pbias[:, NPR:NP]))
            step(dve.tensor_scalar(sign[:, :], alphas[:, :], 1.0, 2.0, ALU.is_le, ALU.mult))
            step(dve.tensor_scalar(sign[:, :], sign[:, :], -1.0, None, ALU.add))
            step(dve.tensor_scalar(unleak[:, :], alphas[:, :], -1.0, 1.0, ALU.mult, ALU.add))
            step(dve.tensor_tensor(colbias[:, 0:3], colbias[:, 0:3], sign[:, 0:3], ALU.mult))
            step(dve.tensor_tensor(leakbias[:, :], colbias[:, 0:3], alphas[:, 0:3], ALU.mult))
            dve.wait_ge(weights_in, 7 * 16)
            dve.wait_ge(consts, CONSTS)
            for t in range(KT):
                w = wqkv[:, t].rearrange("p n o -> p (n o)")
                step(dve.tensor_tensor(w, w, pscale[:, 0:3 * IC], ALU.mult))
            for n in range(3):
                step(dve.tensor_scalar(wqkv[:, :, n, :], wqkv[:, :, n, :], sign[:, n:n + 1], None, ALU.mult))
            step(dve.tensor_scalar(signed_quarter[:, :], signed_quarter[:, :], sign[:, 0:1], sign[:, 1:2], ALU.mult, ALU.mult))
            v_rows = wconv[0:3 * IC].rearrange("p d k o -> p (d k o)")
            step(dve.tensor_scalar(v_rows, v_rows, sign[0:3 * IC, 2:3], None, ALU.mult))
            for d in range(ND):
                cols = slice(3 * IC + d * IC, 3 * IC + (d + 1) * IC)
                for kw in range(3):
                    w = wconv[0:3 * IC, d, kw]
                    step(dve.tensor_tensor(w, w, pscale[0:3 * IC, cols], ALU.mult))
                step(dve.tensor_copy(wconv[3 * IC:3 * IC + 1, d, 0], pbias[3 * IC:3 * IC + 1, cols]))
            step(dve.tensor_tensor(wout[:, :], wout[:, :], pscale[0:NB, 3 * IC + NB:NPR], ALU.mult))
            assert steps[0] == SETUP_STEPS
            dve.wait_ge(pads_out, PAD_DMAS * 16)

            def keep_qkv(b, s, i, m):
                p = qkv_ps[m]
                dve.wait_ge(leak_ready, (b * NCH + s) * 3 + 3)
                for n, img in enumerate((q_img, k_img)):
                    dve.scalar_tensor_tensor(
                        out=img[:, :, bass.ds(s * R, R)],
                        in0=p[:, n * PX:(n + 1) * PX].rearrange("p (h w) -> p w h", h=R), scalar=colbias[:, n:n + 1],
                        in1=leak[:, m, n * PX:(n + 1) * PX].rearrange("p (h w) -> p w h", h=R),
                        op0=ALU.add, op1=ALU.max).then_inc(qk_kept, 1)
                dve.wait_ge(v_out[m], (b * NH + i) * 16 + 16)
                dve.scalar_tensor_tensor(
                    out=vbuf[:, m, PAD:PAD + W], in0=p[:, 2 * PX:3 * PX], scalar=colbias[:, 2:3],
                    in1=leak[:, m, 2 * PX:3 * PX], op0=ALU.add, op1=ALU.max).then_inc(v_kept, 1)

            def rows_to_qkv(b):
                with dve.Fori(0, NH) as i:
                    for m in (0, 1):
                        keep_qkv(b, 2 * i + m, i, m)

            def row_max(U, m):
                for n, (a, z) in enumerate(((0, SQ), (SQ, NQ))):
                    dve.wait_ge(s_done, U * 2 + (n + 5))
                    dve.tensor_reduce(nmax[:, m, a:z], s_ps[n][:, 0:H * (z - a)].rearrange("p (q j) -> p q j", j=H),
                                      AX_X, ALU.max, negate=True).then_inc(max_done, 1)

            def keep_probT(U, m):
                dve.wait_ge(exp_done, U * NQ + 2 * NQ)
                for g in range(G):
                    quarter = slice(IC * g, IC * g + IC)
                    turned = dve.transpose(probT[quarter, m, NQ:2 * NQ, quarter], prob[quarter, m, :, 128:H])
                turned.then_inc(pt_kept, 1)
                dve.wait_ge(pt_done, U * 2 + 2)
                dve.tensor_copy(probT[:, m, FIRST], pt_ps[1][:, 0:128]).then_inc(pt_kept, 1)

            def normalise(b, U, i, m):
                dve.wait_ge(pv_done, U + 3)
                pv = pv_ps[:, 0:NQ * NV].rearrange("p (q n) -> p q n", n=NV)
                dve.reciprocal(rden[:, m], pv[:, :, NB]).then_inc(den_done, 1)
                dve.wait_ge(den_done, U + 1)
                dve.wait_ge(att_out[m], (b * NH + i) * (ND * 16) + 16)
                dve.tensor_tensor(obuf[:, m].rearrange("p r q c -> p q r c"),
                                  pv[:, :, 0:NB].rearrange("p q (r c) -> p q r c", r=ND),
                                  rden[:, m].unsqueeze(2).unsqueeze(3).to_broadcast([128, NQ, ND, IC]),
                                  ALU.mult).then_inc(o_kept, 1)

            def residual(V, k, i, n, m):
                if n == 0:
                    dve.wait_ge(xb_in[m], (k * NH + i + 1) * 16)
                    dve.wait_ge(z_out[m], (k * NH + i) * 16 + 16)
                rows = slice(2 * W * n, 2 * W * n + 2 * W)
                for f in range(KT):
                    dve.wait_ge(pr_done, V * 4 + (2 * n + f + 2))
                    dve.scalar_tensor_tensor(out=zbuf[:, m, f, rows], in0=pr_ps[f][:, 0:2 * W],
                                             scalar=colbias[:, 3 + f:4 + f], in1=xbuf[:, m, f, rows],
                                             op0=ALU.add, op1=ALU.add).then_inc(z_added, 1)

            def prelu_out(V, m):
                dve.wait_ge(r_ready, V + 1)
                z = zbuf[:, m].rearrange("p t n -> p (t n)")
                dve.scalar_tensor_tensor(out=z, in0=rbuf[:, :], scalar=unleak[:, 3:4], in1=z,
                                         op0=ALU.mult, op1=ALU.add).then_inc(z_done, 1)

            def slot(b, u, i, m, k, first=False, last=False):
                U = b * NCH + u
                if not last:
                    row_max(U + 1, 1 - m)
                if k is not None:
                    residual(k * NCH + u, k, i, 0, m)
                keep_probT(U, m)
                if k is not None:
                    residual(k * NCH + u, k, i, 1, m)
                    prelu_out(k * NCH + u, m)
                if not first:
                    normalise(b, U - 1, i + (m - 1), 1 - m)

            def columns(b, k=None):
                row_max(b * NCH, 0)
                slot(b, 0, 0, 0, k, first=True)
                slot(b, 1, 0, 1, k)
                with dve.Fori(1, NH - 1) as i:
                    for m in (0, 1):
                        slot(b, 2 * i + m, i, m, k)
                slot(b, NCH - 2, NH - 1, 0, k)
                slot(b, NCH - 1, NH - 1, 1, k, last=True)
                normalise(b, b * NCH + (NCH - 1), NH - 1, 1)

            with dve.Fori(0, LEAD) as b:
                rows_to_qkv(b)
                columns(b)
            with dve.Fori(0, B - LEAD) as k:
                rows_to_qkv(k + LEAD)
                columns(k + LEAD, k)

            def last_residual(T, i, m):
                dve.wait_ge(last_x_in[m], i * 16 + 16)
                dve.wait_ge(last_z_out[m], i * 16 + 16)
                for n in range(2):
                    for f in range(KT):
                        dve.wait_ge(last_pr_done, T * 4 + (2 * n + f + 1))
                        part = slice(f * R * W + 2 * W * n, f * R * W + 2 * W * n + 2 * W)
                        dve.scalar_tensor_tensor(out=ring_z[:, m, part], in0=ps[4 + 2 * n + f][:, 0:2 * W],
                                                 scalar=colbias[:, 3 + f:4 + f], in1=ring_x[:, m, part],
                                                 op0=ALU.add, op1=ALU.add).then_inc(last_added, 1)

            def last_prelu(T, m):
                dve.wait_ge(last_r_ready, T + 1)
                dve.scalar_tensor_tensor(out=ring_z[:, m], in0=ring_r[:, m % 2], scalar=unleak[:, 3:4], in1=ring_z[:, m],
                                         op0=ALU.mult, op1=ALU.add).then_inc(last_z_done, 1)

            LOOPS = NCH // RING
            with dve.Fori(0, LEAD) as n:
                last_residual(n * NCH, n * LOOPS, 0)
                with dve.Fori(0, LOOPS - 1) as i:
                    for m in range(RING):
                        T = n * NCH + RING * i + m
                        last_residual(T + 1, n * LOOPS + i + (m + 1) // RING, (m + 1) % RING)
                        last_prelu(T, m)
                for v in range(NCH - RING, NCH):
                    if v + 1 < NCH:
                        last_residual(n * NCH + (v + 1), n * LOOPS + (LOOPS - 1), (v + 1) % RING)
                    last_prelu(n * NCH + v, v % RING)

        @block.scalar
        def _(act):
            act.wait_ge(setup_dve, 2)
            act.activation(proot, pinv, ACT.Sqrt).then_inc(setup_root, 1)
            act.wait_ge(params_in, 48)
            act.wait_ge(setup_dve, SETUP_STEPS)
            act.wait_ge(consts, CONSTS)

            def leak_qkv(b, s, m):
                act.wait_ge(qkv_done, b * NCH + s + 3)
                act.wait_ge(v_kept, b * NCH + s + 1)
                for n in range(3):
                    act.activation(leak[:, m, n * PX:(n + 1) * PX], qkv_ps[m][:, n * PX:(n + 1) * PX], ACT.Identity,
                                   bias=leakbias[:, n:n + 1], scale=alphas[:, n:n + 1]).then_inc(leak_ready, 1)

            def store_v(b, s, m):
                act.wait_ge(v_kept, b * NCH + s + 3)
                rows = bass.AP(
                    tensor=vpad.tensor,
                    offset=vpad.offset + b * (IC * HP * WP) + s * (R * WP) + PAD * WP,
                    ap=[[WP, R], [HP * WP, IC], [1, WP]])
                act.dma_start(rows, vbuf[:, m]).then_inc(v_out[m], 16)

            def keep_conv(b, s, m):
                act.wait_ge(conv_done, b * NCH + s + 3)
                act.activation(t_img[:, :, :, bass.ds(s * R, R)],
                               conv_ps[m][:, 0:ND * PX].rearrange("p (d h w) -> p w d h", d=ND, h=R),
                               ACT.Relu).then_inc(conv_kept, 1)

            def rows_to_qkvt(b):
                leak_qkv(b, 0, 0)
                for s in range(1, LAG):
                    leak_qkv(b, s, s % 2)
                    store_v(b, s - 1, (s - 1) % 2)
                with act.Fori(0, NH - LAG // 2) as i:
                    for m in (0, 1):
                        leak_qkv(b, 2 * i + (m + LAG), m)
                        store_v(b, 2 * i + (m + LAG - 1), 1 - m)
                        keep_conv(b, 2 * i + m, m)
                store_v(b, NCH - 1, 1)
                for s in range(NCH - LAG, NCH):
                    keep_conv(b, s, s % 2)

            def keep_first_tiles(U, m):
                act.wait_ge(pt_done, U * 2 + 1)
                act.activation(probT[:, m, 0:FIRST].rearrange("p a i -> p (a i)"), pt_ps[0][:, :], ACT.Copy).then_inc(pa_kept, 1)

            def store_attended(b, u, m):
                act.wait_ge(o_kept, b * NCH + u + 2)
                for r in range(ND):
                    rows = bass.AP(
                        tensor=att.tensor,
                        offset=att.offset + b * (W * H * IC) + u * (H * IC) + r * (B * W * H * IC),
                        ap=[[WG * H * IC, G], [NQ * IC, IC], [1, NQ * IC]])
                    act.dma_start(rows, obuf[:, m, r].rearrange("p q c -> p (q c)")).then_inc(att_out[m], 16)

            def store_out(k, v, m):
                act.wait_ge(z_done, k * NCH + v + 2)
                act.dma_start(out_rows[(3 * k) % B, :, :, bass.ds(v * (R * W), R * W)], zbuf[:, m]).then_inc(z_out[m], 16)

            def exponentials(U, m, between=None):
                for q in range(NQ):
                    if q in (0, SQ):
                        act.wait_ge(max_done, U * 2 + (1 if q == 0 else 2))
                    a, n = (q, 0) if q < SQ else (q - SQ, 1)
                    act.activation(prob[:, m, q], s_ps[n][:, H * a:H * a + H], ACT.Exp,
                                   bias=nmax[:, m, q:q + 1]).then_inc(exp_done, 1)
                    if q == SQ - 1 and between is not None:
                        between()

            def keep_zc(V, m):
                for n in range(2):
                    act.wait_ge((z_turned, zt_turned)[n], V + (1, 3)[n])
                    act.activation(zc[:, m, 2 * W * n:2 * W * n + 2 * W], pr_ps[n][0:NB, 0:2 * W], ACT.Copy).then_inc(zc_kept, 1)

            def negative_part(V, m):
                act.wait_ge(z_added, V * 4 + 12)
                act.wait_ge(z_done, V + 1)
                act.activation(rbuf[:, :], zbuf[:, m].rearrange("p t n -> p (t n)"), ACT.Relu, scale=-1.0).then_inc(r_ready, 1)

            def slot(b, u, m, k, first=False, second=False, last=False):
                U = b * NCH + u
                if k is not None:
                    keep_zc(k * NCH + u, m)
                    if not first:
                        store_out(k, u - 1, 1 - m)
                if last:
                    keep_first_tiles(U, m)
                else:
                    exponentials(U + 1, 1 - m, lambda: keep_first_tiles(U, m))
                if not first and not second:
                    store_attended(b, u - 2, m)
                if k is not None:
                    negative_part(k * NCH + u, m)

            def columns(b, k=None):
                exponentials(b * NCH, 0)
                slot(b, 0, 0, k, first=True)
                slot(b, 1, 1, k, second=True)
                with act.Fori(1, NH - 1) as i:
                    for m in (0, 1):
                        slot(b, 2 * i + m, m, k)
                slot(b, NCH - 2, 0, k)
                slot(b, NCH - 1, 1, k, last=True)
                store_attended(b, NCH - 2, 0)
                store_attended(b, NCH - 1, 1)
                if k is not None:
                    store_out(k, NCH - 1, 1)

            with act.Fori(0, LEAD) as b:
                rows_to_qkvt(b)
                columns(b)
            with act.Fori(0, B - LEAD) as k:
                rows_to_qkvt(k + LEAD)
                columns(k + LEAD, k)

            def last_keep_zc(T, m):
                for n in range(2):
                    act.wait_ge(last_turned, T * 2 + (2 * RING + n + 1))
                    act.activation(ring_zc[:, m % 2, 2 * W * n:2 * W * n + 2 * W], ps[n][0:NB, 0:2 * W],
                                   ACT.Copy).then_inc(last_zc_kept, 1)

            def last_negative_part(T, m):
                act.wait_ge(last_added, T * 4 + (4 * RING + 4))
                act.wait_ge(last_z_done, T + 1)
                act.activation(ring_r[:, m % 2], ring_z[:, m], ACT.Relu, scale=-1.0).then_inc(last_r_ready, 1)

            def last_store(n, T, v, m):
                act.wait_ge(last_z_done, T + 3)
                act.dma_start(out_rows[(3 * n + 3 * (B - LEAD)) % B, :, :, bass.ds(v * (R * W), R * W)],
                              ring_z[:, m].rearrange("p (t n) -> p t n", t=KT)).then_inc(last_z_out[m], 16)

            with act.Fori(0, LEAD) as n:
                first = n * NCH
                last_keep_zc(first, 0)
                last_keep_zc(first + 1, 1)
                last_negative_part(first, 0)
                with act.Fori(0, NCH // RING - 1) as i:
                    for m in range(RING):
                        v = RING * i + m
                        last_keep_zc(first + v + 2, m + 2)
                        last_store(n, first + v, v, m)
                        last_negative_part(first + v + 1, (m + 1) % RING)
                for v in range(NCH - RING, NCH):
                    if v + 2 < NCH:
                        last_keep_zc(first + (v + 2), v % RING + 2)
                    last_store(n, first + v, v, v % RING)
                    if v + 1 < NCH:
                        last_negative_part(first + (v + 1), (v + 1) % RING)
            for m in range(RING):
                act.wait_ge(last_z_out[m], LEAD * (NCH // RING) * 16 + 16)
            for m in (0, 1):
                act.wait_ge(z_out[m], (B - LEAD) * NH * 16 + 16)
                act.wait_ge(v_out[m], B * NH * 16 + 16)
                act.wait_ge(att_out[m], B * NH * ND * 16 + 16)


_BN = ("gamma", "beta", "mean", "var")


def kernel(**inputs):
    import concourse.bacc as bacc
    from concourse.bass_utils import run_bass_kernel_spmd

    p = {n[len("L0_conv_"):]: np.asarray(a) for n, a in inputs.items() if n != "x"}
    convs = ("d1", "d2", "d3")
    row = np.stack([np.concatenate([p[f"{n}_{s}"] for n in ("q", "k", "v") + convs + ("o",)]) for s in _BN])
    col = np.stack([np.stack([np.tile(p[f"{n}_{s}"], G) for n in ("q", "k", "v")]
                             + list(p[f"o_{s}"].reshape(KT, 128)), axis=-1) for s in _BN], axis=1)
    arrays = {
        "x": np.asarray(inputs["x"]),
        "wq": p["q_w"].T, "wk": p["k_w"].T, "wv": p["v_w"].T,
        **{f"w{n}": p[f"{n}_w"].transpose(1, 2, 3, 0).reshape(3 * IC, 3, IC) for n in convs},
        "wo": p["o_w"].T,
        "bn_row": row, "bn_col": col,
        "alpha": np.concatenate([p[f"{n}_alpha"] for n in ("q", "k", "v", "o")]),
    }
    arrays = {n: np.ascontiguousarray(a) for n, a in arrays.items()}
    nc = bacc.Bacc("TRN2", target_bir_lowering=False, num_devices=1)
    aps = [nc.dram_tensor(n, list(a.shape), mybir.dt.from_np(a.dtype), kind="ExternalInput").ap() for n, a in arrays.items()]
    out = nc.dram_tensor("out", [B, C, H, W], F32, kind="ExternalOutput").ap()
    build(nc, *aps, out)
    r = run_bass_kernel_spmd(nc, [arrays], core_ids=[0])
    return r.results[0]["out"]
```
